# Optimizing a Trainium2 kernel written in Bass

```python
import numpy as np
import jax
import jax.numpy as jnp

def _softmax(x, axis=-1):
    return jax.nn.softmax(x, axis=axis)

def _gelu(x):
    return jax.nn.gelu(x, approximate=True)

def _silu(x):
    return jax.nn.silu(x)

def _sigmoid(x):
    return jax.nn.sigmoid(x)

def _layernorm(x, axis=-1, eps=1e-05):
    m = jnp.mean(x, axis=axis, keepdims=True)
    v = jnp.var(x, axis=axis, keepdims=True)
    return (x - m) / jnp.sqrt(v + eps)

def _scatter_add(tgt, idx, src, axis=0):
    return tgt.at[idx].add(src)

def _segment_sum(src, seg, n):
    return jax.ops.segment_sum(src, seg, n)
kernel_name = 'mk_lm_tower_d1_tok_ids1024_r4_1e805e'

def setup_inputs(seed: int=0):
    np.random.seed(seed)
    _w = jnp.asarray

    def _rec_inputs():
        import jax
        import jax.numpy as jnp
        _rk = jax.random.key(seed)
        x = jax.random.randint(jax.random.fold_in(_rk, 1), (64, 128), 0, 12564, jnp.int32)
        return x
    x = _rec_inputs()

    def _L0_tok_setup():
        import jax, jax.numpy as jnp
        import numpy as np
        VOCAB, EMBED_DIM, R = (50257, 256, 16)
        ALPHA = 32
        BATCH, SEQ = (8, 1024)
        key = jax.random.key(seed)
        k1, k2, k3, k4 = jax.random.split(key, 4)
        x = jax.random.randint(k1, (BATCH, SEQ), 0, VOCAB, dtype=jnp.int64)
        W = jax.random.normal(k2, (VOCAB, EMBED_DIM), dtype=jnp.float32)
        A = jax.random.normal(k3, (VOCAB, R), dtype=jnp.float32) * 0.01
        B = jax.random.normal(k4, (R, EMBED_DIM), dtype=jnp.float32)
        return {'x': x, 'W': W, 'A': A, 'B': B}
    _L0_tok_all = _L0_tok_setup()
    _L0_tok_in = {k: v for k, v in _L0_tok_all.items() if k in ('W', 'A', 'B')}
    del _L0_tok_all

    def _L0_attn_setup():
        import jax, jax.numpy as jnp
        import numpy as np
        D_MODEL = 256
        NUM_HEADS = 16
        DK = D_MODEL // NUM_HEADS
        key = jax.random.key(seed)
        kx, kq, kk, kv, ko = jax.random.split(key, 5)
        B, S = (4, 512)
        bound = float(np.sqrt(6.0 / (D_MODEL + D_MODEL)))
        uni = lambda k: jax.random.uniform(k, (D_MODEL, D_MODEL), jnp.float32, -bound, bound)
        return {'x': jax.random.normal(kx, (B, S, D_MODEL), jnp.float32), 'q_heads': uni(kq), 'k_heads': uni(kk), 'v_heads': uni(kv), 'output_proj': uni(ko)}
    _L0_attn_all = _L0_attn_setup()
    _L0_attn_in = {k: v for k, v in _L0_attn_all.items() if k in ('q_heads', 'k_heads', 'v_heads', 'output_proj')}
    del _L0_attn_all

    def _L0_ffn_setup():
        import jax, jax.numpy as jnp
        import numpy as np
        E = 16
        G = 4
        EPG = E // G
        K = 4
        TOPK_GROUP = 2
        PER_GROUP_K = K // TOPK_GROUP

        def _route(xf, router_w, correction_bias):
            S = xf.shape[0]
            logits = xf @ router_w.T
            scores = jax.nn.sigmoid(logits)
            sb = scores + correction_bias
            grp_top = jax.lax.top_k(sb.reshape(S, G, EPG), PER_GROUP_K)[0]
            group_scores = grp_top.sum(axis=-1)
            _, group_idx = jax.lax.top_k(group_scores, TOPK_GROUP)
            group_mask = jnp.zeros((S, G), sb.dtype).at[jnp.arange(S)[:, None], group_idx].set(1.0)
            score_mask = jnp.broadcast_to(group_mask[:, :, None], (S, G, EPG)).reshape(S, E)
            masked = jnp.where(score_mask > 0, sb, -jnp.inf)
            _, topk_idx = jax.lax.top_k(masked, K)
            w = jnp.take_along_axis(scores, topk_idx, axis=1)
            w = w / (w.sum(axis=-1, keepdims=True) + 1e-20)
            return (topk_idx, w, scores)
        key = jax.random.key(seed)
        ks = jax.random.split(key, 9)
        B, T, C, H, HS = (2, 256, 256, 64, 512)
        std = 0.02
        return {'x': jax.random.normal(ks[0], (B, T, C), jnp.float32), 'router_w': jax.random.normal(ks[1], (E, C), jnp.float32) * std, 'correction_bias': jnp.zeros((E,), jnp.float32), 'gate_w': jax.random.normal(ks[2], (E, C, H), jnp.float32) * std, 'up_w': jax.random.normal(ks[3], (E, C, H), jnp.float32) * std, 'down_w': jax.random.normal(ks[4], (E, H, C), jnp.float32) * std, 'shared_gate_w': jax.random.normal(ks[5], (HS, C), jnp.float32) * std, 'shared_up_w': jax.random.normal(ks[6], (HS, C), jnp.float32) * std, 'shared_down_w': jax.random.normal(ks[7], (C, HS), jnp.float32) * std}
    _L0_ffn_all = _L0_ffn_setup()
    _L0_ffn_in = {k: v for k, v in _L0_ffn_all.items() if k in ('router_w', 'correction_bias', 'gate_w', 'up_w', 'down_w', 'shared_gate_w', 'shared_up_w', 'shared_down_w')}
    del _L0_ffn_all
    return {'x': x, 'L0_tok_W': _L0_tok_in['W'], 'L0_tok_A': _L0_tok_in['A'], 'L0_tok_B': _L0_tok_in['B'], 'L0_attn_q_heads': _L0_attn_in['q_heads'], 'L0_attn_k_heads': _L0_attn_in['k_heads'], 'L0_attn_v_heads': _L0_attn_in['v_heads'], 'L0_attn_output_proj': _L0_attn_in['output_proj'], 'L0_ffn_router_w': _L0_ffn_in['router_w'], 'L0_ffn_correction_bias': _L0_ffn_in['correction_bias'], 'L0_ffn_gate_w': _L0_ffn_in['gate_w'], 'L0_ffn_up_w': _L0_ffn_in['up_w'], 'L0_ffn_down_w': _L0_ffn_in['down_w'], 'L0_ffn_shared_gate_w': _L0_ffn_in['shared_gate_w'], 'L0_ffn_shared_up_w': _L0_ffn_in['shared_up_w'], 'L0_ffn_shared_down_w': _L0_ffn_in['shared_down_w']}

def reference(x, L0_tok_W, L0_tok_A, L0_tok_B, L0_attn_q_heads, L0_attn_k_heads, L0_attn_v_heads, L0_attn_output_proj, L0_ffn_router_w, L0_ffn_correction_bias, L0_ffn_gate_w, L0_ffn_up_w, L0_ffn_down_w, L0_ffn_shared_gate_w, L0_ffn_shared_up_w, L0_ffn_shared_down_w):
    import jax
    import jax.numpy as jnp

    def _L0_tok_ref(x, W, A, B):
        import jax, jax.numpy as jnp
        import numpy as np
        VOCAB, EMBED_DIM, R = (50257, 256, 16)
        ALPHA = 32
        BATCH, SEQ = (8, 1024)
        scale = ALPHA / R
        origin_out = W[x]
        lora_out = scale * (A[x] @ B)
        return origin_out + lora_out

    def _L0_attn_ref(x, q_heads, k_heads, v_heads, output_proj):
        import jax, jax.numpy as jnp
        import numpy as np
        D_MODEL = 256
        NUM_HEADS = 16
        DK = D_MODEL // NUM_HEADS
        B, S, _ = x.shape

        def proj(W):
            return (x @ W.T).reshape(B, S, NUM_HEADS, DK).transpose(0, 2, 1, 3)
        q, k, v = (proj(q_heads), proj(k_heads), proj(v_heads))
        scale = 1.0 / jnp.sqrt(jnp.asarray(DK, x.dtype))
        scores = jnp.einsum('bhqd,bhkd->bhqk', q, k) * scale
        causal = jnp.triu(jnp.ones((S, S), bool), k=1)
        scores = jnp.where(causal, jnp.asarray(-jnp.inf, scores.dtype), scores)
        attn = jax.nn.softmax(scores, axis=-1)
        out = jnp.einsum('bhqk,bhkd->bhqd', attn, v)
        out = out.transpose(0, 2, 1, 3).reshape(B, S, D_MODEL)
        return out @ output_proj.T

    def _L0_ffn_ref(x, router_w, correction_bias, gate_w, up_w, down_w, shared_gate_w, shared_up_w, shared_down_w):
        import jax, jax.numpy as jnp
        import numpy as np
        E = 16
        G = 4
        EPG = E // G
        K = 4
        TOPK_GROUP = 2
        PER_GROUP_K = K // TOPK_GROUP

        def _route(xf, router_w, correction_bias):
            S = xf.shape[0]
            logits = xf @ router_w.T
            scores = jax.nn.sigmoid(logits)
            sb = scores + correction_bias
            grp_top = jax.lax.top_k(sb.reshape(S, G, EPG), PER_GROUP_K)[0]
            group_scores = grp_top.sum(axis=-1)
            _, group_idx = jax.lax.top_k(group_scores, TOPK_GROUP)
            group_mask = jnp.zeros((S, G), sb.dtype).at[jnp.arange(S)[:, None], group_idx].set(1.0)
            score_mask = jnp.broadcast_to(group_mask[:, :, None], (S, G, EPG)).reshape(S, E)
            masked = jnp.where(score_mask > 0, sb, -jnp.inf)
            _, topk_idx = jax.lax.top_k(masked, K)
            w = jnp.take_along_axis(scores, topk_idx, axis=1)
            w = w / (w.sum(axis=-1, keepdims=True) + 1e-20)
            return (topk_idx, w, scores)
        B, T, C = x.shape
        S = B * T
        xf = x.reshape(S, C)
        sg = xf @ shared_gate_w.T
        su = xf @ shared_up_w.T
        shared_out = jax.nn.silu(sg) * su @ shared_down_w.T
        topk_idx, w, _scores = _route(xf, router_w, correction_bias)
        combine = jnp.zeros((S, E), xf.dtype).at[jnp.arange(S)[:, None], topk_idx].add(w)
        g = jnp.einsum('sc,ech->esh', xf, gate_w)
        u = jnp.einsum('sc,ech->esh', xf, up_w)
        h = jax.nn.silu(g) * u
        hw = h * combine.T[:, :, None]
        routed = jnp.einsum('esh,ehc->sc', hw, down_w)
        return (shared_out + routed).reshape(B, T, C)
    h = _L0_tok_ref(x, L0_tok_W, L0_tok_A, L0_tok_B)
    h = h + _L0_attn_ref(_layernorm(h, axis=-1), L0_attn_q_heads, L0_attn_k_heads, L0_attn_v_heads, L0_attn_output_proj)
    h = h + _L0_ffn_ref(_layernorm(h, axis=-1), L0_ffn_router_w, L0_ffn_correction_bias, L0_ffn_gate_w, L0_ffn_up_w, L0_ffn_down_w, L0_ffn_shared_gate_w, L0_ffn_shared_up_w, L0_ffn_shared_down_w)
    return h

_drawn_inputs = setup_inputs


def setup_inputs(seed=0):
    import zlib

    import numpy as np

    out = dict(_drawn_inputs(seed))
    spreads = {'L0_ffn_correction_bias': (0.0, 0.8)}
    factors = {'L0_ffn_router_w': 8.0,
     'L0_ffn_gate_w': 8.0,
     'L0_ffn_up_w': 8.0,
     'L0_ffn_down_w': 8.0,
     'L0_ffn_shared_gate_w': 8.0,
     'L0_ffn_shared_up_w': 8.0,
     'L0_ffn_shared_down_w': 8.0}
    for name, (base, spread) in spreads.items():
        noise = np.random.default_rng([zlib.crc32(name.encode()), seed]).standard_normal(out[name].shape)
        drawn = base * np.exp(spread * noise) if base else spread * noise
        out[name] = jnp.asarray(drawn.astype(out[name].dtype))
    for name, factor in factors.items():
        out[name] = (out[name] * factor).astype(out[name].dtype)
    return out
```

```python
from contextlib import ExitStack

import numpy as np

import concourse.bass as bass
from concourse import mybir

ALU = mybir.AluOpType
ACT = mybir.ActivationFunctionType
AX_X = mybir.AxisListType.X
F32 = mybir.dt.float32
F32R = mybir.dt.float32r
I32 = mybir.dt.int32

P = 128
SEQS = 64
PAIRS = SEQS // 2
D = 256
KC = D // P
HEADS = 16
DK = D // HEADS
RANK = 16
LORA_SCALE = 2.0
EPS = 1e-5
E = 16
EG = 4
HID = 16 * 64 + 512
CH = HID // P
CH_ROUTED = 16 * 64 // P
GT = 4
GROUPS = SEQS // GT
TOK = GT * P
NEVER = 3.0e38
W_COLS = 3 * CH * D
PIECE = W_COLS // PAIRS

PASSES = ((0, 0), (0, 1), (1, 0))


def need(eng, sem, count):
    if not isinstance(count, int) or count > 0:
        eng.wait_ge(sem, count)


def need_before(eng, met, met_count, *counts):
    counts = [(sem, n if isinstance(n, int) else eng.compute_val(n)) for sem, n in counts]
    eng.wait_ge(met, met_count)
    for sem, n in counts:
        need(eng, sem, n)


def slot(g, c, e):
    return 4 * g + 2 * c + e


def build(nc, idx_d, emb_d, lora_a_d, lora_b_d, attn_w_d, ffn_w_d, router_d, bias_d, ident_d, const_d, sel_d, out_d):
    with ExitStack() as whole:
        def keep(name, shape, dt=F32):
            return whole.enter_context(nc.sbuf_tensor(name, shape, dt))

        h = keep("h", [P, SEQS, D])
        ffn_hi = keep("ffn_hi", [P, W_COLS], F32R)
        ffn_lo = keep("ffn_lo", [P, W_COLS], F32R)
        ident = keep("ident", [P, P])

        with ExitStack() as ctx:
            attention_block(nc, ctx, h, ffn_hi, ffn_lo, ident, idx_d, emb_d, lora_a_d, lora_b_d, attn_w_d, ffn_w_d,
                            ident_d, const_d)
        with ExitStack() as ctx:
            expert_block(nc, ctx, h, ffn_hi, ffn_lo, ident, router_d, bias_d, sel_d, out_d)


def attention_block(nc, ctx, h, ffn_hi, ffn_lo, ident, idx_d, emb_d, lora_a_d, lora_b_d, attn_w_d, ffn_w_d,
                    ident_d, const_d):
    def sb(name, shape, dt=F32):
        return ctx.enter_context(nc.sbuf_tensor(name, shape, dt))

    def bank(name):
        return ctx.enter_context(nc.psum_tensor(name, [P, 512], F32))

    def sem(name):
        return ctx.enter_context(nc.semaphore(name))

    mask = sb("mask", [P, P])
    parity = sb("parity", [P, 2])
    head_sel = sb("head_sel", [HEADS, KC, P])
    idx = sb("idx", [P, SEQS], I32)
    lora_b = sb("lora_b", [RANK, D])
    attn_w = sb("attn_w", [P, 2, 4, KC, D], F32R)
    piece = sb("piece", [P, PIECE])
    minus_half = sb("minus_half", [P, 2])
    idx_pair = sb("idx_pair", [P, 2], I32)
    emb_rows = sb("emb_rows", [P, 2, D])
    a_rows = sb("a_rows", [P, 2, P])
    a_T = sb("a_T", [RANK, 2 * P])
    stats = sb("stats", [P, 2, 6])
    mean_var = sb("mean_var", [P, 2, 2])
    var_eps = sb("var_eps", [P, 2])
    rstd = sb("rstd", [P, 2])
    xn = sb("xn", [P, 2, D])
    xT = sb("xT", [P, 2, KC, 2 * P], F32R)
    qT = sb("qT", [P, 2, KC, 2 * P], F32R)
    kT = sb("kT", [P, 2, KC, 2, 2 * P], F32R)
    v_wide = sb("v_wide", [P, 2, HEADS, 2 * DK])
    probs = sb("probs", [P, HEADS, P])
    neg_max = sb("neg_max", [P, HEADS])
    sums = sb("sums", [P, HEADS])
    recip = sb("recip", [P, P])
    recip_T = sb("recip_T", [HEADS, P])
    recip_rows = sb("recip_rows", [P, KC * P])
    probs_T = sb("probs_T", [P, HEADS, P])
    attn = sb("attn", [P, KC * P])
    attn_r = sb("attn_r", [P, 2, KC * P], F32R)

    scores_ps = [bank(f"scores_ps{g}") for g in range(4)]
    turn_ps = [bank(f"turn_ps{k}") for k in range(2)]
    attn_ps = bank("attn_ps")
    misc_ps = bank("misc_ps")

    const_in, b_in, w_in, idx_in = sem("const_in"), sem("b_in"), sem("w_in"), sem("idx_in")
    rows_in, piece_in = sem("rows_in"), sem("piece_in")
    zeros_set, b_scaled, w_hi, w_lo = sem("zeros_set"), sem("b_scaled"), sem("w_hi"), sem("w_lo")
    idx_copied, rstd_ready, piece_hi, piece_lo = sem("idx_copied"), sem("rstd_ready"), sem("piece_hi"), sem("piece_lo")
    scores_done, turned, recip_turned, attn_done = sem("scores_done"), sem("turned"), sem("recip_turned"), sem("attn_done")
    a_turned, lora_done, v_done, x_turned = sem("a_turned"), sem("lora_done"), sem("v_done"), sem("x_turned")
    q_done, k_done, out_done = sem("q_done"), sem("k_done"), sem("out_done")
    masked, turn_odd_out, recip_done, recip_T_out = sem("masked"), sem("turn_odd_out"), sem("recip_done"), sem("recip_T_out")
    recip_rows_out, attn_normed, attn_hi, attn_lo = sem("recip_rows_out"), sem("attn_normed"), sem("attn_hi"), sem("attn_lo")
    a_out, embedded, stats_done, mv_done = sem("a_out"), sem("embedded"), sem("stats_done"), sem("mv_done")
    eps_added, normed, x_lo, q_lo, k_lo, added = (sem("eps_added"), sem("normed"), sem("x_lo"), sem("q_lo"),
                                                  sem("k_lo"), sem("added"))
    exps, turn_even_out, v_out, x_hi, q_hi, k_hi = (sem("exps"), sem("turn_even_out"), sem("v_out"), sem("x_hi"),
                                                    sem("q_hi"), sem("k_hi"))

    block = ctx.enter_context(nc.Block())

    @block.sync
    def _(sp):
        sp.dma_start(idx[:], idx_d).then_inc(idx_in, 16)
        sp.dma_start(ident[:], ident_d).then_inc(const_in, 16)
        sp.dma_start(probs[:].rearrange("p a b -> p (a b)"), attn_w_d).then_inc(w_in, 16)
        sp.dma_start(lora_b[:], lora_b_d).then_inc(b_in, 16)
        sp.dma_start(mask[:], const_d[:, 0:P]).then_inc(const_in, 16)
        sp.dma_start(parity[:], const_d[:, P:P + 2]).then_inc(const_in, 16)
        sp.dma_start(head_sel[:], const_d[0:HEADS, P + 2:P + 2 + KC * P].rearrange("h (c m) -> h c m", c=KC)
                     ).then_inc(const_in, 16)
        sp.dma_start(piece[:], ffn_w_d[:, 0:PIECE]).then_inc(piece_in, 16)
        with sp.Fori(1, PAIRS) as i:
            sp.wait_ge(piece_lo, i)
            sp.dma_start(piece[:], ffn_w_d[:, bass.ds(i * PIECE, PIECE)]).then_inc(piece_in, 16)

    @block.gpsimd
    def _(pool):
        def gather(pair):
            need(pool, embedded, 2 * pair)
            nc.gpsimd.tensor_copy(idx_pair[:], idx[:, bass.ds(2 * pair, 2)]).then_inc(idx_copied, 1)
            need_before(pool, idx_in, 16, (idx_copied, pair + 1))
            for s in range(2):
                at = bass.IndirectOffsetOnAxis(ap=idx_pair[:, s:s + 1], axis=0)
                nc.gpsimd.indirect_dma_start(out=emb_rows[:, s, :], out_offset=None, in_=emb_d,
                                             in_offset=at).then_inc(rows_in, 16)
                nc.gpsimd.indirect_dma_start(out=a_rows[:, s, 0:RANK], out_offset=None, in_=lora_a_d,
                                             in_offset=at).then_inc(rows_in, 16)

        def root(pair):
            pool.wait_ge(eps_added, pair + 1)
            nc.gpsimd.tensor_tensor(rstd[:], var_eps[:], minus_half[:], ALU.pow).then_inc(rstd_ready, 1)

        def split_piece(i):
            at = bass.ds(i * PIECE, PIECE)
            pool.wait_ge(piece_in, 16 * (i + 1))
            nc.gpsimd.tensor_copy(ffn_hi[:, at], piece[:]).then_inc(piece_hi, 1)
            pool.wait_ge(piece_hi, i + 1)
            nc.gpsimd.tensor_tensor(ffn_lo[:, at], piece[:], ffn_hi[:, at].bitcast(F32),
                                    ALU.subtract).then_inc(piece_lo, 1)

        nc.gpsimd.memset(a_rows[:], 0.0).then_inc(zeros_set, 1)
        nc.gpsimd.memset(minus_half[:], -0.5).then_inc(zeros_set, 1)
        nc.gpsimd.memset(v_wide[:], 0.0).then_inc(zeros_set, 1)
        nc.gpsimd.memset(recip[:], 0.0).then_inc(zeros_set, 1)
        pool.wait_ge(zeros_set, 4)
        pool.wait_ge(idx_in, 16)
        gather(0)
        root(0)
        gather(1)

        def body(i, last=False, gathers=True):
            if not last:
                root(i + 1)
            if gathers:
                gather(i + 2)
            split_piece(i)

        body(0)
        with pool.Fori(1, PAIRS - 2) as i:
            body(i)
        body(PAIRS - 2, gathers=False)
        body(PAIRS - 1, last=True, gathers=False)

    @block.tensor
    def _(pe):
        def turn_a(pair):
            pe.wait_ge(rows_in, 64 * (pair + 1))
            need(pe, added, 2 * pair - 3)
            for s in range(2):
                mm = nc.tensor.transpose(misc_ps[:, s * P:(s + 1) * P], a_rows[:, s, :], ident[:])
            mm.then_inc(a_turned, 1)

        def lora(pair):
            pe.wait_ge(a_out, pair + 1)
            need(pe, turn_odd_out, 4 * (pair - 1))
            for s in range(2):
                mm = nc.tensor.matmul(turn_ps[1][:, s * D:(s + 1) * D], a_T[:, s * P:(s + 1) * P], lora_b[:],
                                      start=True, stop=True)
            mm.then_inc(lora_done, 1)

        def turn_x(pair):
            pe.wait_ge(normed, 2 * pair + 2)
            need(pe, added, 2 * pair - 2)
            pe.wait_ge(a_out, pair + 1)
            for s in range(2):
                for k in range(KC):
                    mm = nc.tensor.transpose(misc_ps[:, (2 * k + s) * P:(2 * k + s + 1) * P],
                                             xn[:, s, k * P:(k + 1) * P], ident[:])
            mm.then_inc(x_turned, 1)

        def project(pair, w, ps):
            for m in range(KC):
                for k in range(KC):
                    for n, (a, b) in enumerate(PASSES):
                        mm = nc.tensor.matmul(ps[:, m * D:(m + 1) * D], attn_w[:, a, w, k, m * P:(m + 1) * P],
                                              xT[:, b, k, :], start=(k == 0 and n == 0),
                                              stop=(k == KC - 1 and n == 2))
            return mm

        def project_qk(pair):
            pe.wait_ge(x_hi, pair + 1)
            pe.wait_ge(x_lo, pair + 1)
            need(pe, turn_even_out, 4 * pair - 2)
            project(pair, 0, turn_ps[0]).then_inc(q_done, 1)
            need(pe, turn_odd_out, 4 * pair - 2)
            pe.wait_ge(embedded, 2 * pair + 2)
            project(pair, 1, turn_ps[1]).then_inc(k_done, 1)

        def project_v(pair):
            need(pe, turn_even_out, 4 * pair)
            pe.wait_ge(q_hi, pair + 1)
            pe.wait_ge(q_lo, pair + 1)
            for s in range(2):
                for k in range(KC):
                    for n, (a, b) in enumerate(PASSES):
                        mm = nc.tensor.matmul(turn_ps[0][:, s * D:(s + 1) * D], xT[:, a, k, s * P:(s + 1) * P],
                                              attn_w[:, b, 2, k, :], start=(k == 0 and n == 0),
                                              stop=(k == KC - 1 and n == 2))
            mm.then_inc(v_done, 1)

        def scores(n, s):
            for half in range(2):
                groups = (2 * half, 2 * half + 1)
                for g in groups:
                    need(pe, masked, 4 * n - 3 + g)
                for c in range(KC):
                    for t, (a, b) in enumerate(PASSES):
                        for g in groups:
                            r = 32 * g
                            mm = nc.tensor.matmul(
                                scores_ps[g][:, c * 2 * P:(c + 1) * 2 * P].rearrange("p (e k) -> p e k", e=2),
                                qT[r:r + 32, a, c, s * P:(s + 1) * P], kT[r:r + 32, b, c, :, s * P:(s + 1) * P],
                                start=(t == 0), stop=(t == 2))
                            if c == KC - 1 and t == 2:
                                mm.then_inc(scores_done, 1)

        def turn_probs(n, extra):
            for g in range(4):
                pe.wait_ge(exps, 4 * n + g + 1)
                if g < 2:
                    extra(g)
                elif g == 2:
                    pe.wait_ge(turn_even_out, 2 * n + 1)
                else:
                    pe.wait_ge(turn_odd_out, 2 * n + 1)
                for j in range(4):
                    mm = nc.tensor.transpose(turn_ps[g % 2][:, j * P:(j + 1) * P], probs[:, 4 * g + j, :], ident[:])
                mm.then_inc(turned, 1)
            pe.wait_ge(recip_done, n + 1)
            need(pe, attn_normed, n)
            nc.tensor.transpose(attn_ps[:, D:D + P], recip[:], ident[:]).then_inc(recip_turned, 1)

        def attend(n, s):
            pe.wait_ge(recip_T_out, n + 1)
            pe.wait_ge(turn_even_out, 2 * n + 2)
            pe.wait_ge(turn_odd_out, 2 * n + 2)
            for c in range(KC):
                nc.tensor.matmul(attn_ps[:, D + c * P:D + (c + 1) * P], head_sel[:, c, :], recip_T[:],
                                 start=True, stop=True)
            for c in range(KC):
                for e in range(2):
                    for g in range(4):
                        mm = nc.tensor.matmul(attn_ps[32 * g:32 * g + 32, c * P:(c + 1) * P],
                                              v_wide[:, s, 8 * c + 2 * g + e, :], probs_T[:, slot(g, c, e), :],
                                              start=(e == 0), stop=(e == 1))
            mm.then_inc(attn_done, 1)

        def project_out(n, extra):
            pe.wait_ge(attn_lo, n + 1)
            extra()
            for c in range(KC):
                for t, (a, b) in enumerate(PASSES):
                    mm = nc.tensor.matmul(misc_ps[:, 0:D], attn_r[:, a, c * P:(c + 1) * P], attn_w[:, b, 3, c, :],
                                          start=(c == 0 and t == 0), stop=(c == KC - 1 and t == 2))
            mm.then_inc(out_done, 1)

        pe.wait_ge(const_in, 64)
        pe.wait_ge(zeros_set, 4)
        turn_a(0)
        pe.wait_ge(b_scaled, 1)
        lora(0)
        turn_x(0)
        pe.wait_ge(w_hi, 1)
        pe.wait_ge(w_lo, 1)
        project_qk(0)

        def body(i, first=False, last=False):
            a, b, before, pair = 2 * i, 2 * i + 1, 2 * i - 1, i + 1

            def q_read(g):
                if g == 0:
                    pe.wait_ge(q_hi, pair + 1)
                    pe.wait_ge(q_lo, pair + 1)
                else:
                    pe.wait_ge(k_hi, pair + 1)
                    pe.wait_ge(k_lo, pair + 1)

            def v_read(g):
                if g == 0:
                    pe.wait_ge(v_out, i + 1)
                elif last:
                    pe.wait_ge(turn_odd_out, 4 * i)
                else:
                    pe.wait_ge(embedded, 2 * pair + 2)

            def last_read(g):
                if g == 0:
                    pe.wait_ge(turn_even_out, 2 * a + 2)
                else:
                    pe.wait_ge(turn_odd_out, 2 * a + 2)

            def x_read():
                pe.wait_ge(x_hi, pair + 1)
                pe.wait_ge(x_lo, pair + 1)

            pe.wait_ge(q_hi, i + 1)
            pe.wait_ge(q_lo, i + 1)
            pe.wait_ge(k_hi, i + 1)
            pe.wait_ge(k_lo, i + 1)
            scores(a, 0)
            if not first:
                attend(before, 1)
            if not last:
                turn_a(pair)
            project_v(i)
            if not last:
                lora(pair)
            if not first:
                if last:
                    project_out(before, lambda: pe.wait_ge(added, a - 1))
                else:
                    project_out(before, lambda: pe.wait_ge(a_out, pair + 1))
            turn_probs(a, v_read)
            if not last:
                turn_x(pair)
            scores(b, 1)
            attend(a, 0)
            if not last:
                project_qk(pair)
                project_out(a, x_read)
                turn_probs(b, q_read)
            else:
                project_out(a, lambda: pe.wait_ge(added, a))
                turn_probs(b, last_read)

        body(0, first=True)
        with pe.Fori(1, PAIRS - 1) as i:
            body(i)
        body(PAIRS - 1, last=True)
        attend(SEQS - 1, 1)
        project_out(SEQS - 1, lambda: pe.wait_ge(added, SEQS - 1))

    @block.vector
    def _(dve):
        def mask_scores(n):
            for g in range(4):
                need_before(dve, w_lo, 1, (scores_done, 4 * n + g + 1), (turned, 4 * n - 3 + g))
                for j in range(4):
                    last = nc.vector.tensor_tensor_reduce(
                        probs[:, 4 * g + j, :], scores_ps[g][:, j * P:(j + 1) * P], mask[:], 1.0, NEVER,
                        ALU.add, ALU.min, neg_max[:, 4 * g + j:4 * g + j + 1])
                last.then_inc(masked, 1)

        def invert_sums(n):
            dve.wait_ge(exps, 4 * n + 4)
            need(dve, recip_turned, n)
            nc.vector.reciprocal(recip[:, 0:HEADS], sums[:]).then_inc(recip_done, 1)

        def turn_recip(n):
            dve.wait_ge(recip_turned, n + 1)
            need(dve, attn_done, n)
            nc.vector.tensor_copy(recip_T[:], attn_ps[0:HEADS, D:D + P]).then_inc(recip_T_out, 1)

        def norm_attention(n):
            dve.wait_ge(attn_done, n + 1)
            nc.vector.tensor_copy(recip_rows[:], attn_ps[:, D:2 * D]).then_inc(recip_rows_out, 1)
            dve.wait_ge(recip_rows_out, n + 1)
            nc.vector.tensor_tensor(attn[:], attn_ps[:, 0:D], recip_rows[:], ALU.mult).then_inc(attn_normed, 1)
            dve.wait_ge(attn_normed, n + 1)
            need(dve, out_done, n)
            nc.vector.tensor_copy(attn_r[:, 0, :], attn[:]).then_inc(attn_hi, 1)
            dve.wait_ge(attn_hi, n + 1)
            nc.vector.tensor_tensor(attn_r[:, 1, :], attn[:], attn_r[:, 0, :].bitcast(F32),
                                    ALU.subtract).then_inc(attn_lo, 1)

        def copy_a(pair):
            dve.wait_ge(a_turned, pair + 1)
            need(dve, lora_done, pair)
            nc.vector.tensor_copy(a_T[:], misc_ps[0:RANK, 0:2 * P]).then_inc(a_out, 1)

        def embed(pair):
            dve.wait_ge(lora_done, pair + 1)
            dve.wait_ge(rows_in, 64 * (pair + 1))
            for s in range(2):
                n = 2 * pair + s
                nc.vector.tensor_tensor(h[:, n, :], turn_ps[1][:, s * D:(s + 1) * D], emb_rows[:, s, :],
                                        ALU.add).then_inc(embedded, 1)
            for s in range(2):
                n = 2 * pair + s
                need_before(dve, w_lo, 1, (embedded, n + 1))
                nc.vector.bn_stats(stats[:, s, :], h[:, n, :]).then_inc(stats_done, 1)
            for s in range(2):
                n = 2 * pair + s
                need_before(dve, w_lo, 1, (stats_done, n + 1))
                nc.vector.bn_aggr(mean_var[:, s, :], stats[:, s, :]).then_inc(mv_done, 1)
            dve.wait_ge(mv_done, 2 * pair + 2)
            need(dve, rstd_ready, pair)
            nc.vector.tensor_scalar(var_eps[:], mean_var[:, :, 1], EPS, None, ALU.add).then_inc(eps_added, 1)

        def norm(pair):
            dve.wait_ge(rstd_ready, pair + 1)
            need(dve, x_turned, pair)
            for s in range(2):
                n = 2 * pair + s
                nc.vector.tensor_scalar(xn[:, s, :], h[:, n, :], mean_var[:, s, 0:1], rstd[:, s:s + 1],
                                        ALU.subtract, ALU.mult).then_inc(normed, 1)

        def add_attention(n):
            dve.wait_ge(out_done, n + 1)
            nc.vector.tensor_tensor(h[:, n, :], misc_ps[:, 0:D], h[:, n, :], ALU.add).then_inc(added, 1)

        def copy_turned(n):
            for k, g in enumerate((1, 3)):
                dve.wait_ge(turned, 4 * n + g + 1)
                need(dve, attn_done, n)
                nc.vector.tensor_copy(probs_T[:, 4 * g:4 * g + 4, :],
                                      turn_ps[1][:].rearrange("p (j q) -> p j q", j=4)).then_inc(turn_odd_out, 1)

        def low_x(pair):
            dve.wait_ge(x_turned, pair + 1)
            dve.wait_ge(x_hi, pair + 1)
            need(dve, v_done, pair)
            nc.vector.tensor_tensor(xT[:, 1].rearrange("p k n -> p (k n)"), misc_ps[:],
                                    xT[:, 0].rearrange("p k n -> p (k n)").bitcast(F32),
                                    ALU.subtract).then_inc(x_lo, 1)

        def low_qk(pair):
            need(dve, scores_done, 8 * pair)
            dve.wait_ge(q_hi, pair + 1)
            nc.vector.scalar_tensor_tensor(out=qT[:, 1], in0=turn_ps[0][:].rearrange("p (c n) -> p c n", c=KC),
                                           scalar=-DK ** -0.5, in1=qT[:, 0].bitcast(F32), op0=ALU.mult,
                                           op1=ALU.subtract).then_inc(q_lo, 1)
            dve.wait_ge(k_hi, pair + 1)
            for e in range(2):
                last = nc.vector.scalar_tensor_tensor(
                    out=kT[:, 1, :, e, :], in0=turn_ps[1][:].rearrange("p (c n) -> p c n", c=KC),
                    scalar=parity[:, e:e + 1], in1=kT[:, 0, :, e, :].bitcast(F32), op0=ALU.mult, op1=ALU.subtract)
            last.then_inc(k_lo, 1)

        dve.wait_ge(b_in, 16)
        nc.vector.tensor_scalar(lora_b[:], lora_b[:], LORA_SCALE, None, ALU.mult).then_inc(b_scaled, 1)
        dve.wait_ge(w_hi, 1)
        nc.vector.tensor_tensor(attn_w[:, 1].rearrange("p w k n -> p (w k n)"), probs[:].rearrange("p a b -> p (a b)"),
                                attn_w[:, 0].rearrange("p w k n -> p (w k n)").bitcast(F32),
                                ALU.subtract).then_inc(w_lo, 1)
        dve.wait_ge(const_in, 64)
        dve.wait_ge(zeros_set, 4)
        dve.wait_ge(w_lo, 1)
        copy_a(0)
        embed(0)
        norm(0)
        low_x(0)
        low_qk(0)

        def body(i, first=False, last=False):
            a, b, before, pair = 2 * i, 2 * i + 1, 2 * i - 1, i + 1
            mask_scores(a)
            if not first:
                norm_attention(before)
            if not last:
                copy_a(pair)
                embed(pair)
            if not first:
                add_attention(before)
            if not last:
                norm(pair)
            invert_sums(a)
            copy_turned(a)
            turn_recip(a)
            if not last:
                low_x(pair)
            mask_scores(b)
            norm_attention(a)
            if not last:
                low_qk(pair)
            add_attention(a)
            invert_sums(b)
            copy_turned(b)
            turn_recip(b)

        body(0, first=True)
        with dve.Fori(1, PAIRS - 1) as i:
            body(i)
        body(PAIRS - 1, last=True)
        norm_attention(SEQS - 1)
        add_attention(SEQS - 1)

    @block.scalar
    def _(act):
        def exponents(n):
            for g in range(4):
                act.wait_ge(masked, 4 * n + g + 1)
                if g == 0:
                    need(act, recip_done, n)
                for j in range(4 * g, 4 * g + 4):
                    last = nc.scalar.activation(probs[:, j, :], probs[:, j, :], ACT.Exp, bias=neg_max[:, j:j + 1],
                                                scale=-1.0, accum_out=sums[:, j:j + 1])
                last.then_inc(exps, 1)

        def copy_turned(n):
            for g in (0, 2):
                act.wait_ge(turned, 4 * n + g + 1)
                need(act, attn_done, n)
                nc.scalar.activation(probs_T[:, 4 * g:4 * g + 4, :],
                                     turn_ps[0][:].rearrange("p (j q) -> p j q", j=4), ACT.Copy
                                     ).then_inc(turn_even_out, 1)

        def widen_v(pair):
            act.wait_ge(v_done, pair + 1)
            need(act, attn_done, 2 * pair)
            for e in range(2):
                last = nc.scalar.activation(
                    v_wide[:].rearrange("p s (j e) w -> p (s j) e w", e=2)[:, :, e, e * DK:(e + 1) * DK],
                    turn_ps[0][:].rearrange("p (x e w) -> p x e w", e=2, w=DK)[:, :, e, :], ACT.Copy)
            last.then_inc(v_out, 1)

        def high_x(pair):
            act.wait_ge(x_turned, pair + 1)
            need(act, v_done, pair)
            nc.scalar.activation(xT[:, 0].rearrange("p k n -> p (k n)"), misc_ps[:], ACT.Copy).then_inc(x_hi, 1)

        def high_qk(pair):
            act.wait_ge(q_done, pair + 1)
            need(act, scores_done, 8 * pair)
            nc.scalar.activation(qT[:, 0], turn_ps[0][:].rearrange("p (c n) -> p c n", c=KC), ACT.Copy,
                                 scale=-DK ** -0.5).then_inc(q_hi, 1)
            act.wait_ge(k_done, pair + 1)
            for e in range(2):
                last = nc.scalar.activation(kT[:, 0, :, e, :], turn_ps[1][:].rearrange("p (c n) -> p c n", c=KC),
                                            ACT.Copy, scale=parity[:, e:e + 1])
            last.then_inc(k_hi, 1)

        act.wait_ge(w_in, 16)
        nc.scalar.activation(attn_w[:, 0].rearrange("p w k n -> p (w k n)"), probs[:].rearrange("p a b -> p (a b)"),
                             ACT.Copy).then_inc(w_hi, 1)
        act.wait_ge(const_in, 64)
        act.wait_ge(zeros_set, 4)
        high_x(0)
        high_qk(0)

        def body(i, last=False):
            a, b, pair = 2 * i, 2 * i + 1, i + 1
            exponents(a)
            widen_v(i)
            copy_turned(a)
            if not last:
                high_x(pair)
            exponents(b)
            if not last:
                high_qk(pair)
            copy_turned(b)

        body(0)
        with act.Fori(1, PAIRS - 1) as i:
            body(i)
        body(PAIRS - 1, last=True)


def expert_block(nc, ctx, h, ffn_hi, ffn_lo, ident, router_d, bias_d, sel_d, out_d):
    def sb(name, shape, dt=F32):
        return ctx.enter_context(nc.sbuf_tensor(name, shape, dt))

    def bank(name):
        return ctx.enter_context(nc.psum_tensor(name, [P, 512], F32))

    def sem(name):
        return ctx.enter_context(nc.semaphore(name))

    parts = [w[:].rearrange("p (t n) -> p t n", t=3) for w in (ffn_hi, ffn_lo)]
    gate_w = [w[:, 0, :].rearrange("p (k n) -> p k n", k=KC) for w in parts]
    up_w = [w[:, 1, :].rearrange("p (k n) -> p k n", k=KC) for w in parts]
    down_w = [w[:, 2, :].rearrange("p (c n) -> p c n", c=CH) for w in parts]

    router_raw = sb("router_raw", [P, KC, P])
    router_w = sb("router_w", [P, 2, KC, P], F32R)
    expert_sel_raw = sb("expert_sel_raw", [2 * E, CH_ROUTED, P])
    expert_sel = sb("expert_sel", [2 * E, CH_ROUTED, P], F32R)
    bias = sb("bias", [P, E])
    earlier = sb("earlier", [P, E, E])
    minus_half = sb("minus_half2", [P, GT])
    stats = sb("stats2", [P, GT, 6])
    mean_var = sb("mean_var2", [P, GT, 2])
    var_eps = sb("var_eps2", [P, GT])
    rstd = sb("rstd2", [P, GT])
    xn = sb("xn2", [P, GT, D])
    xT = sb("xT2", [P, 2, 2, KC, TOK], F32R)
    score_T = sb("score_T", [E, TOK])
    score = sb("score", [P, GT, E])
    biased = sb("biased", [P, GT, E])
    pair_sums = sb("pair_sums", [P, GT, EG, 6])
    group_score = sb("group_score", [P, GT, EG])
    beats = sb("beats", [P, 2, E, E])
    ties = sb("ties", [P, 2, E, E])
    group_rank = sb("group_rank", [P, GT, EG])
    group_on = sb("group_on", [P, GT, EG])
    group_off = sb("group_off", [P, GT, EG])
    candidates = sb("candidates", [P, GT, E])
    rank = sb("rank", [P, GT, E])
    weight = sb("weight", [P, GT, E])
    total = sb("total", [P, GT])
    total_inv = sb("total_inv", [P, GT])
    combine = sb("combine", [P, GT, E])
    combine_hi = sb("combine_hi", [P, GT, E], F32R)
    combine_r = sb("combine_r", [P, GT, P])
    combine_T = sb("combine_T", [2 * E, TOK], F32R)
    silu = sb("silu", [P, 2, TOK])
    scaled = sb("scaled", [P, 2, TOK])
    hid = sb("hid", [P, 2, TOK])
    hid_hi = sb("hid_hi", [P, 2, TOK], F32R)
    hid_lo = sb("hid_lo", [P, 2, TOK], F32R)

    gate_ps = [bank(f"gate_ps{k}") for k in range(2)]
    up_ps = [bank(f"up_ps{k}") for k in range(2)]
    combine_ps = bank("combine_ps")
    out_ps = [bank(f"out_ps{k}") for k in range(2)]
    misc_ps = bank("misc_ps2")

    const_in, stored = sem("const2_in"), sem("stored")
    zeros_set, rstd_ready = sem("zeros2_set"), sem("rstd2_ready")
    x_turned, logits_done, score_turned, combine_turned = (sem("x2_turned"), sem("logits_done"), sem("score_turned"),
                                                           sem("combine_turned"))
    gate_done, up_done, spread_done, down_done = sem("gate_done"), sem("up_done"), sem("spread_done"), sem("down_done")
    router_lo, eps_added, normed, x_lo = sem("router_lo"), sem("eps2_added"), sem("normed2"), sem("x2_lo")
    combine_hi_done = sem("combine_hi_done")
    step, score_out, combined, scaled_done = sem("step"), sem("score_out"), sem("combined"), sem("scaled_done")
    hid_done, hid_lo_done, y_done = sem("hid_done"), sem("hid_lo_done"), sem("y_done")
    consts_cast, x_hi, scored, combine_T_out = sem("consts_cast"), sem("x2_hi"), sem("scored"), sem("combine_T_out")
    silu_done, hid_hi_done = sem("silu_done"), sem("hid_hi_done")

    block = ctx.enter_context(nc.Block())
    out_rows = out_d.rearrange("(t p) d -> p t d", p=P)


    @block.sync
    def _(sp):
        sp.dma_start(router_raw[:], router_d).then_inc(const_in, 16)
        sp.dma_start(expert_sel_raw[:], sel_d).then_inc(const_in, 16)
        sp.dma_start(bias[:], bias_d).then_inc(const_in, 16)

        with sp.Fori(0, GROUPS) as g:
            sp.wait_ge(y_done, 2 * g + 2)
            sp.dma_start(out_rows[:, bass.ds(GT * g, GT), :], h[:, bass.ds(GT * g, GT), :]).then_inc(stored, 16)
        sp.wait_ge(stored, 16 * GROUPS)

    @block.gpsimd
    def _(pool):
        nc.gpsimd.memset(combine_r[:], 0.0).then_inc(zeros_set, 1)
        nc.gpsimd.memset(minus_half[:], -0.5).then_inc(zeros_set, 1)
        nc.gpsimd.memset(earlier[:], 1.0).then_inc(zeros_set, 1)
        pool.wait_ge(zeros_set, 3)
        nc.gpsimd.affine_select(out=earlier[:], in_=earlier[:], compare_op=ALU.is_gt, fill=0.0, base=0,
                                pattern=[[1, E], [-1, E]], channel_multiplier=0).then_inc(zeros_set, 1)

        def root(g):
            pool.wait_ge(eps_added, g + 1)
            nc.gpsimd.tensor_tensor(rstd[:], var_eps[:], minus_half[:], ALU.pow).then_inc(rstd_ready, 1)

        with pool.Fori(0, GROUPS) as g:
            root(g)

    @block.tensor
    def _(pe):
        def turn_x(g, k):
            pe.wait_ge(normed, g + 1)
            if k == 0:
                need(pe, combine_T_out, g)
            else:
                pe.wait_ge(x_hi, 2 * g + 1)
                pe.wait_ge(x_lo, 2 * g + 1)
            for t in range(GT):
                mm = nc.tensor.transpose(misc_ps[:, t * P:(t + 1) * P], xn[:, t, k * P:(k + 1) * P], ident[:])
            mm.then_inc(x_turned, 1)

        def logits(g, parity):
            pe.wait_ge(x_hi, 2 * g + 2)
            pe.wait_ge(x_lo, 2 * g + 2)
            for k in range(KC):
                for n, (a, b) in enumerate(PASSES):
                    mm = nc.tensor.matmul(misc_ps[:], router_w[:, a, k, :], xT[:, parity, b, k, :],
                                          start=(k == 0 and n == 0), stop=(k == KC - 1 and n == 2))
            mm.then_inc(logits_done, 1)

        def turn_scores(g):
            need_before(pe, zeros_set, 4, (scored, g + 1))
            for t in range(GT):
                mm = nc.tensor.transpose(misc_ps[:, t * E:(t + 1) * E], score_T[:, t * P:(t + 1) * P],
                                         ident[0:E, 0:E])
            mm.then_inc(score_turned, 1)

        def turn_combine(g):
            pe.wait_ge(combined, g + 1)
            pe.wait_ge(score_out, g + 1)
            for t in range(GT):
                mm = nc.tensor.transpose(misc_ps[:, t * P:(t + 1) * P], combine_r[:, t, :], ident[:])
            mm.then_inc(combine_turned, 1)

        def spread(g, c):
            if c == 0:
                pe.wait_ge(combine_T_out, g + 1)
            need(pe, scaled_done, CH_ROUTED * g + c)
            nc.tensor.matmul(combine_ps[:], expert_sel[:, c, :], combine_T[:], start=True,
                             stop=True).then_inc(spread_done, 1)

        def up_or_gate(g, parity, c, w, ps):
            for k in range(KC):
                for n, (a, b) in enumerate(PASSES):
                    mm = nc.tensor.matmul(ps[:], w[a][:, k, c * P:(c + 1) * P], xT[:, parity, b, k, :],
                                          start=(k == 0 and n == 0), stop=(k == KC - 1 and n == 2))
            return mm

        def down(g, c):
            pe.wait_ge(hid_hi_done, CH * g + c + 1)
            pe.wait_ge(hid_lo_done, CH * g + c + 1)
            hid_r = (hid_hi, hid_lo)
            for t in range(GT):
                if c == 0 and t % 2 == 0:
                    need(pe, y_done, 2 * g - 1 + t // 2)
                for n, (a, b) in enumerate(PASSES):
                    mm = nc.tensor.matmul(out_ps[t // 2][:, (t % 2) * D:(t % 2 + 1) * D],
                                          hid_r[a][:, c % 2, t * P:(t + 1) * P], down_w[b][:, c, :],
                                          start=(c == 0 and n == 0 and t % 2 == 0),
                                          stop=(c == CH - 1 and n == 2), skip_group_check=True)
            mm.then_inc(down_done, 1)

        def experts(g, parity, first=False, route=True):
            for c in range(CH):
                if c < CH_ROUTED:
                    spread(g, c)
                need(pe, silu_done, CH * g + c - 1)
                up_or_gate(g, parity, c, gate_w, gate_ps[c % 2]).then_inc(gate_done, 1)
                need(pe, hid_done, CH * g + c - 1)
                up_or_gate(g, parity, c, up_w, up_ps[c % 2]).then_inc(up_done, 1)
                if route and c in (2, 4):
                    turn_x(g + 1, (c - 2) // 2)
                if route and c == 6:
                    logits(g + 1, 1 - parity)
                if route and c == 8:
                    turn_scores(g + 1)
                if route and c == 11:
                    turn_combine(g + 1)
                if c > 0:
                    down(g, c - 1)
                elif not first:
                    down(g - 1, CH - 1)

        pe.wait_ge(consts_cast, 2)
        pe.wait_ge(router_lo, 1)
        pe.wait_ge(zeros_set, 4)
        turn_x(0, 0)
        turn_x(0, 1)
        logits(0, 0)
        turn_scores(0)
        turn_combine(0)
        experts(0, 0, first=True)
        with pe.Fori(0, GROUPS // 2 - 1) as j:
            experts(2 * j + 1, 1)
            experts(2 * j + 2, 0)
        experts(GROUPS - 1, 1, route=False)
        down(GROUPS - 1, CH - 1)

    @block.vector
    def _(dve):
        STEPS = 26

        def norm_rows(g):
            for t in range(GT):
                last = nc.vector.bn_stats(stats[:, t, :], h[:, GT * g + t, :])
            last.then_inc(step, 1)
            need_before(dve, zeros_set, 4, (step, STEPS * g + 1))
            for t in range(GT):
                last = nc.vector.bn_aggr(mean_var[:, t, :], stats[:, t, :])
            last.then_inc(step, 1)
            dve.wait_ge(step, STEPS * g + 2)
            nc.vector.tensor_scalar(var_eps[:], mean_var[:, :, 1], EPS, None, ALU.add).then_inc(eps_added, 1)
            dve.wait_ge(rstd_ready, g + 1)
            need(dve, x_turned, 2 * g)
            for t in range(GT):
                last = nc.vector.tensor_scalar(xn[:, t, :], h[:, GT * g + t, :], mean_var[:, t, 0:1],
                                               rstd[:, t:t + 1], ALU.subtract, ALU.mult)
            last.then_inc(normed, 1)

        def low_x(g, parity, k):
            dve.wait_ge(x_turned, 2 * g + k + 1)
            dve.wait_ge(x_hi, 2 * g + k + 1)
            nc.vector.tensor_tensor(xT[:, parity, 1, k, :], misc_ps[:], xT[:, parity, 0, k, :].bitcast(F32),
                                    ALU.subtract).then_inc(x_lo, 1)

        def route(g):
            done = [2]

            def then(last):
                done[0] += 1
                last.then_inc(step, 1)
                dve.wait_ge(step, STEPS * g + done[0])

            tt = nc.vector.tensor_tensor
            dve.wait_ge(score_turned, g + 1)
            nc.vector.tensor_copy(score[:], misc_ps[:, 0:GT * E].rearrange("p (t e) -> p t e", t=GT)
                                  ).then_inc(score_out, 1)
            dve.wait_ge(score_out, g + 1)
            then(tt(biased[:], score[:], bias[:].unsqueeze(1).to_broadcast([P, GT, E]), ALU.add))
            b4 = biased[:].rearrange("p t (g i) -> p t g i", g=EG)
            at = 0
            for d in (1, 2, 3):
                last = tt(pair_sums[:, :, :, at:at + 4 - d], b4[:, :, :, 0:4 - d], b4[:, :, :, d:4], ALU.add)
                at += 4 - d
            then(last)
            then(nc.vector.tensor_reduce(group_score[:], pair_sums[:], AX_X, ALU.max))
            gs = group_score[:]
            gi = gs.unsqueeze(3).to_broadcast([P, GT, EG, EG])
            gj = gs.unsqueeze(2).to_broadcast([P, GT, EG, EG])
            more = beats[:, 0, 0:GT, :].rearrange("p t (i j) -> p t i j", i=EG)
            same = ties[:, 0, 0:GT, :].rearrange("p t (i j) -> p t i j", i=EG)
            early = earlier[:, 0:EG, 0:EG].unsqueeze(1).to_broadcast([P, GT, EG, EG])
            tt(more, gj, gi, ALU.is_gt)
            then(tt(same, gj, gi, ALU.is_equal))
            then(tt(same, same, early, ALU.mult))
            then(tt(more, more, same, ALU.add))
            then(nc.vector.tensor_reduce(group_rank[:], more, AX_X, ALU.add))
            nc.vector.tensor_scalar(group_on[:], group_rank[:], 1.5, None, ALU.is_lt)
            then(nc.vector.tensor_scalar(group_off[:], group_rank[:], 1.5, -NEVER, ALU.is_gt, ALU.mult))
            c4 = candidates[:].rearrange("p t (g i) -> p t g i", g=EG)
            then(tt(c4, b4, group_on[:].unsqueeze(3).to_broadcast([P, GT, EG, 4]), ALU.mult))
            then(tt(c4, c4, group_off[:].unsqueeze(3).to_broadcast([P, GT, EG, 4]), ALU.add))
            early = earlier[:].unsqueeze(1).to_broadcast([P, 2, E, E])
            for half in range(2):
                cs = candidates[:, 2 * half:2 * half + 2, :]
                ci = cs.unsqueeze(3).to_broadcast([P, 2, E, E])
                cj = cs.unsqueeze(2).to_broadcast([P, 2, E, E])
                tt(beats[:], cj, ci, ALU.is_gt)
                then(tt(ties[:], cj, ci, ALU.is_equal))
                then(tt(ties[:], ties[:], early, ALU.mult))
                then(tt(beats[:], beats[:], ties[:], ALU.add))
                then(nc.vector.tensor_reduce(rank[:, 2 * half:2 * half + 2, :], beats[:], AX_X, ALU.add))
            then(nc.vector.tensor_scalar(rank[:], rank[:], 3.5, None, ALU.is_lt))
            then(tt(weight[:], score[:], rank[:], ALU.mult))
            then(nc.vector.tensor_reduce(total[:], weight[:], AX_X, ALU.add))
            then(nc.vector.tensor_scalar(total[:], total[:], 1e-20, None, ALU.add))
            then(nc.vector.reciprocal(total_inv[:], total[:]))
            need(dve, combine_turned, g)
            then(tt(combine[:], weight[:], total_inv[:].unsqueeze(2).to_broadcast([P, GT, E]), ALU.mult))
            assert done[0] == STEPS, done
            return tt

        def split_combine(g):
            nc.vector.tensor_copy(combine_hi[:], combine[:]).then_inc(combine_hi_done, 1)
            dve.wait_ge(combine_hi_done, g + 1)
            nc.vector.tensor_copy(combine_r[:, :, 0:E], combine_hi[:].bitcast(F32))
            nc.vector.tensor_tensor(combine_r[:, :, E:2 * E], combine[:], combine_hi[:].bitcast(F32),
                                    ALU.subtract).then_inc(combined, 1)

        def hidden(g, c):
            dve.wait_ge(silu_done, CH * g + c + 1)
            n = CH * g + c
            if c < CH_ROUTED:
                dve.wait_ge(spread_done, CH_ROUTED * g + c + 1)
                nc.vector.tensor_tensor(scaled[:, c % 2, :], combine_ps[:], silu[:, c % 2, :],
                                        ALU.mult).then_inc(scaled_done, 1)
                dve.wait_ge(scaled_done, CH_ROUTED * g + c + 1)
                left = scaled
            else:
                left = silu
            dve.wait_ge(up_done, n + 1)
            need(dve, hid_hi_done, n - 1)
            nc.vector.tensor_tensor(hid[:, c % 2, :], up_ps[c % 2][:], left[:, c % 2, :], ALU.mult
                                    ).then_inc(hid_done, 1)
            dve.wait_ge(hid_done, n + 1)
            dve.wait_ge(hid_hi_done, n + 1)
            nc.vector.tensor_tensor(hid_lo[:, c % 2, :], hid[:, c % 2, :], hid_hi[:, c % 2, :].bitcast(F32),
                                    ALU.subtract).then_inc(hid_lo_done, 1)

        def finish(g):
            dve.wait_ge(down_done, CH * g + CH)
            for k in range(2):
                rows = h[:, bass.ds(GT * g + 2 * k, 2), :]
                nc.vector.tensor_tensor(rows, out_ps[k][:].rearrange("p (t d) -> p t d", t=2), rows,
                                        ALU.add).then_inc(y_done, 1)

        def experts(g, parity, first=False, routes=True):
            for c in range(CH):
                if routes and c == 0:
                    norm_rows(g + 1)
                hidden(g, c)
                if c == 0 and not first:
                    finish(g - 1)
                if routes and c in (2, 4):
                    low_x(g + 1, 1 - parity, (c - 2) // 2)
                if routes and c == 8:
                    route(g + 1)
                    split_combine(g + 1)

        dve.wait_ge(const_in, 48)
        dve.wait_ge(zeros_set, 4)
        dve.wait_ge(consts_cast, 2)
        nc.vector.tensor_tensor(router_w[:, 1], router_raw[:], router_w[:, 0].bitcast(F32),
                                ALU.subtract).then_inc(router_lo, 1)
        norm_rows(0)
        low_x(0, 0, 0)
        low_x(0, 0, 1)
        route(0)
        split_combine(0)
        experts(0, 0, first=True)
        with dve.Fori(0, GROUPS // 2 - 1) as j:
            experts(2 * j + 1, 1)
            experts(2 * j + 2, 0)
        experts(GROUPS - 1, 1, routes=False)
        finish(GROUPS - 1)

    @block.scalar
    def _(act):
        def high_x(g, parity, k):
            act.wait_ge(x_turned, 2 * g + k + 1)
            need(act, up_done, CH * (g - 1))
            nc.scalar.activation(xT[:, parity, 0, k, :], misc_ps[:], ACT.Copy).then_inc(x_hi, 1)

        def score_rows(g):
            act.wait_ge(logits_done, g + 1)
            nc.scalar.activation(score_T[:], misc_ps[0:E, :], ACT.Sigmoid).then_inc(scored, 1)

        def copy_combine(g):
            act.wait_ge(combine_turned, g + 1)
            need(act, spread_done, CH_ROUTED * g)
            nc.scalar.activation(combine_T[:], misc_ps[0:2 * E, :], ACT.Copy).then_inc(combine_T_out, 1)

        def gated(g, c):
            act.wait_ge(gate_done, CH * g + c + 1)
            need(act, hid_done, CH * g + c - 1)
            nc.scalar.activation(silu[:, c % 2, :], gate_ps[c % 2][:], ACT.Silu).then_inc(silu_done, 1)

        def high_hidden(g, c):
            act.wait_ge(hid_done, CH * g + c + 1)
            need(act, down_done, CH * g + c - 1)
            nc.scalar.activation(hid_hi[:, c % 2, :], hid[:, c % 2, :], ACT.Copy).then_inc(hid_hi_done, 1)

        def experts(g, parity, routes=True):
            for c in range(CH):
                gated(g, c)
                high_hidden(g, c)
                if routes and c in (2, 4):
                    high_x(g + 1, 1 - parity, (c - 2) // 2)
                if routes and c == 6:
                    score_rows(g + 1)
                if routes and c == 11:
                    copy_combine(g + 1)

        act.wait_ge(const_in, 48)
        nc.scalar.activation(router_w[:, 0], router_raw[:], ACT.Copy).then_inc(consts_cast, 1)
        nc.scalar.activation(expert_sel[:], expert_sel_raw[:], ACT.Copy).then_inc(consts_cast, 1)
        high_x(0, 0, 0)
        high_x(0, 0, 1)
        score_rows(0)
        copy_combine(0)
        experts(0, 0)
        with act.Fori(0, GROUPS // 2 - 1) as j:
            experts(2 * j + 1, 1)
            experts(2 * j + 2, 0)
        experts(GROUPS - 1, 1, routes=False)




def kernel(x, L0_tok_W, L0_tok_A, L0_tok_B, L0_attn_q_heads, L0_attn_k_heads, L0_attn_v_heads, L0_attn_output_proj,
           L0_ffn_router_w, L0_ffn_correction_bias, L0_ffn_gate_w, L0_ffn_up_w, L0_ffn_down_w, L0_ffn_shared_gate_w,
           L0_ffn_shared_up_w, L0_ffn_shared_down_w):
    from concourse import bacc
    from concourse.bass_utils import run_bass_kernel_spmd

    def chunked(w):
        return np.concatenate(np.split(w, w.shape[0] // P), axis=1)

    attn_w = [chunked(np.asarray(w).T) for w in (L0_attn_q_heads, L0_attn_k_heads, L0_attn_v_heads,
                                                 L0_attn_output_proj)]

    def by_channel(w, shared):
        return chunked(np.concatenate([np.asarray(w).transpose(1, 0, 2).reshape(D, -1), np.asarray(shared).T], axis=1))

    down = np.concatenate([np.asarray(L0_ffn_down_w).reshape(-1, D), np.asarray(L0_ffn_shared_down_w).T], axis=0)
    ffn_w = np.concatenate([by_channel(L0_ffn_gate_w, L0_ffn_shared_gate_w),
                            by_channel(L0_ffn_up_w, L0_ffn_shared_up_w), chunked(down)], axis=1)
    router = np.zeros((KC, P, P), np.float32)
    router[:, :, 0:E] = np.asarray(L0_ffn_router_w).T.reshape(KC, P, E)

    const = np.zeros((P, P + 2 + KC * P), np.float32)
    rows, cols = np.indices((P, P))
    const[:, 0:P] = np.where(cols > rows, np.float32(NEVER), np.float32(0))
    odd = np.arange(P) // DK % 2
    const[:, P] = odd == 0
    const[:, P + 1] = odd == 1
    for c in range(KC):
        for r in range(P):
            const[slot(r // 32, c, r // DK % 2), P + 2 + c * P + r] = 1
    sel = np.zeros((2 * E, CH_ROUTED, P), np.float32)
    for c in range(CH_ROUTED):
        for m in range(P):
            sel[2 * c + m // 64, c, m] = 1
            sel[E + 2 * c + m // 64, c, m] = 1

    arrays = {
        "idx": np.ascontiguousarray(np.asarray(x).T),
        "emb": np.ascontiguousarray(L0_tok_W),
        "lora_a": np.ascontiguousarray(L0_tok_A),
        "lora_b": np.ascontiguousarray(L0_tok_B),
        "attn_w": np.ascontiguousarray(np.concatenate(attn_w, axis=1)),
        "ffn_w": np.ascontiguousarray(ffn_w),
        "router": np.ascontiguousarray(router.transpose(1, 0, 2)),
        "bias": np.ascontiguousarray(np.broadcast_to(np.asarray(L0_ffn_correction_bias), (P, E))),
        "ident": np.eye(P, dtype=np.float32),
        "const": const,
        "sel": sel,
    }
    nc = bacc.Bacc("TRN2", target_bir_lowering=False, num_devices=1)
    args = [nc.dram_tensor(f"in_{name}", a.shape, mybir.dt.from_np(a.dtype), kind="ExternalInput").ap()
            for name, a in arrays.items()]
    out = nc.dram_tensor("out", (SEQS * P, D), F32, kind="ExternalOutput").ap()
    build(nc, *args, out)
    r = run_bass_kernel_spmd(nc, [{f"in_{name}": a for name, a in arrays.items()}], core_ids=[0])
    return r.results[0]["out"].reshape(SEQS, P, D)
```

```python
from contextlib import ExitStack

import numpy as np

import concourse.bass as bass
from concourse import mybir

ALU = mybir.AluOpType
ACT = mybir.ActivationFunctionType
AX_X = mybir.AxisListType.X
F32 = mybir.dt.float32
F32R = mybir.dt.float32r
I32 = mybir.dt.int32

P = 128
SEQS = 64
PAIRS = SEQS // 2
D = 256
KC = D // P
HEADS = 16
DK = D // HEADS
RANK = 16
LORA_SCALE = 2.0
EPS = 1e-5
E = 16
EG = 4
HID = 16 * 64 + 512
CH = HID // P
CH_ROUTED = 16 * 64 // P
GT = 4
GROUPS = SEQS // GT
TOK = GT * P
NEVER = 3.0e38
W_COLS = 3 * CH * D
PIECE = W_COLS // PAIRS

PASSES = ((0, 0), (0, 1), (1, 0))


def need(eng, sem, count):
    if not isinstance(count, int) or count > 0:
        eng.wait_ge(sem, count)


def need_before(eng, met, met_count, *counts):
    counts = [(sem, n if isinstance(n, int) else eng.compute_val(n)) for sem, n in counts]
    eng.wait_ge(met, met_count)
    for sem, n in counts:
        need(eng, sem, n)


def slot(g, c, e):
    return 4 * g + 2 * c + e


def build(nc, idx_d, emb_d, lora_a_d, lora_b_d, attn_w_d, ffn_w_d, router_d, bias_d, ident_d, const_d, sel_d, out_d):
    with ExitStack() as whole:
        def keep(name, shape, dt=F32):
            return whole.enter_context(nc.sbuf_tensor(name, shape, dt))

        h = keep("h", [P, SEQS, D])
        ffn_hi = keep("ffn_hi", [P, W_COLS], F32R)
        ffn_lo = keep("ffn_lo", [P, W_COLS], F32R)
        ident = keep("ident", [P, P])

        with ExitStack() as ctx:
            attention_block(nc, ctx, h, ffn_hi, ffn_lo, ident, idx_d, emb_d, lora_a_d, lora_b_d, attn_w_d, ffn_w_d,
                            ident_d, const_d)
        with ExitStack() as ctx:
            expert_block(nc, ctx, h, ffn_hi, ffn_lo, ident, router_d, bias_d, sel_d, out_d)


def attention_block(nc, ctx, h, ffn_hi, ffn_lo, ident, idx_d, emb_d, lora_a_d, lora_b_d, attn_w_d, ffn_w_d,
                    ident_d, const_d):
    def sb(name, shape, dt=F32):
        return ctx.enter_context(nc.sbuf_tensor(name, shape, dt))

    def bank(name):
        return ctx.enter_context(nc.psum_tensor(name, [P, 512], F32))

    def sem(name):
        return ctx.enter_context(nc.semaphore(name))

    mask = sb("mask", [P, P])
    parity = sb("parity", [P, 2])
    head_sel = sb("head_sel", [HEADS, KC, P])
    idx = sb("idx", [P, SEQS], I32)
    lora_b = sb("lora_b", [RANK, D])
    attn_w = sb("attn_w", [P, 2, 4, KC, D], F32R)
    piece = sb("piece", [P, PIECE])
    minus_half = sb("minus_half", [P, 2])
    idx_pair = sb("idx_pair", [P, 2], I32)
    emb_rows = sb("emb_rows", [P, 2, D])
    a_rows = sb("a_rows", [P, 2, P])
    a_T = sb("a_T", [RANK, 2 * P])
    stats = sb("stats", [P, 2, 6])
    mean_var = sb("mean_var", [P, 2, 2])
    var_eps = sb("var_eps", [P, 2])
    rstd = sb("rstd", [P, 2])
    xn = sb("xn", [P, 2, D])
    xT = sb("xT", [P, 2, KC, 2 * P], F32R)
    qT = sb("qT", [P, 2, KC, 2 * P], F32R)
    kT = sb("kT", [P, 2, KC, 2, 2 * P], F32R)
    v_wide = sb("v_wide", [P, 2, HEADS, 2 * DK])
    probs = sb("probs", [P, HEADS, P])
    neg_max = sb("neg_max", [P, HEADS])
    sums = sb("sums", [P, HEADS])
    recip = sb("recip", [P, P])
    recip_T = sb("recip_T", [HEADS, P])
    recip_rows = sb("recip_rows", [P, KC * P])
    probs_T = sb("probs_T", [P, HEADS, P])
    attn = sb("attn", [P, KC * P])
    attn_r = sb("attn_r", [P, 2, KC * P], F32R)

    scores_ps = [bank(f"scores_ps{g}") for g in range(4)]
    turn_ps = [bank(f"turn_ps{k}") for k in range(2)]
    attn_ps = bank("attn_ps")
    misc_ps = bank("misc_ps")

    const_in, b_in, w_in, idx_in = sem("const_in"), sem("b_in"), sem("w_in"), sem("idx_in")
    rows_in, piece_in = sem("rows_in"), sem("piece_in")
    zeros_set, b_scaled, w_hi, w_lo = sem("zeros_set"), sem("b_scaled"), sem("w_hi"), sem("w_lo")
    idx_copied, rstd_ready, piece_hi, piece_lo = sem("idx_copied"), sem("rstd_ready"), sem("piece_hi"), sem("piece_lo")
    scores_done, turned, recip_turned, attn_done = sem("scores_done"), sem("turned"), sem("recip_turned"), sem("attn_done")
    a_turned, lora_done, v_done, x_turned = sem("a_turned"), sem("lora_done"), sem("v_done"), sem("x_turned")
    q_done, k_done, out_done = sem("q_done"), sem("k_done"), sem("out_done")
    masked, turn_odd_out, recip_done, recip_T_out = sem("masked"), sem("turn_odd_out"), sem("recip_done"), sem("recip_T_out")
    recip_rows_out, attn_normed, attn_hi, attn_lo = sem("recip_rows_out"), sem("attn_normed"), sem("attn_hi"), sem("attn_lo")
    a_out, embedded, stats_done, mv_done = sem("a_out"), sem("embedded"), sem("stats_done"), sem("mv_done")
    eps_added, normed, x_lo, q_lo, k_lo, added = (sem("eps_added"), sem("normed"), sem("x_lo"), sem("q_lo"),
                                                  sem("k_lo"), sem("added"))
    exps, turn_even_out, v_out, x_hi, q_hi, k_hi = (sem("exps"), sem("turn_even_out"), sem("v_out"), sem("x_hi"),
                                                    sem("q_hi"), sem("k_hi"))

    block = ctx.enter_context(nc.Block())

    @block.sync
    def _(sp):
        sp.dma_start(idx[:], idx_d).then_inc(idx_in, 16)
        sp.dma_start(ident[:], ident_d).then_inc(const_in, 16)
        sp.dma_start(probs[:].rearrange("p a b -> p (a b)"), attn_w_d).then_inc(w_in, 16)
        sp.dma_start(lora_b[:], lora_b_d).then_inc(b_in, 16)
        sp.dma_start(mask[:], const_d[:, 0:P]).then_inc(const_in, 16)
        sp.dma_start(parity[:], const_d[:, P:P + 2]).then_inc(const_in, 16)
        sp.dma_start(head_sel[:], const_d[0:HEADS, P + 2:P + 2 + KC * P].rearrange("h (c m) -> h c m", c=KC)
                     ).then_inc(const_in, 16)
        sp.dma_start(piece[:], ffn_w_d[:, 0:PIECE]).then_inc(piece_in, 16)
        with sp.Fori(1, PAIRS) as i:
            sp.wait_ge(piece_lo, i)
            sp.dma_start(piece[:], ffn_w_d[:, bass.ds(i * PIECE, PIECE)]).then_inc(piece_in, 16)

    @block.gpsimd
    def _(pool):
        def gather(pair):
            need(pool, embedded, 2 * pair)
            nc.gpsimd.tensor_copy(idx_pair[:], idx[:, bass.ds(2 * pair, 2)]).then_inc(idx_copied, 1)
            need_before(pool, idx_in, 16, (idx_copied, pair + 1))
            for s in range(2):
                at = bass.IndirectOffsetOnAxis(ap=idx_pair[:, s:s + 1], axis=0)
                nc.gpsimd.indirect_dma_start(out=emb_rows[:, s, :], out_offset=None, in_=emb_d,
                                             in_offset=at).then_inc(rows_in, 16)
                nc.gpsimd.indirect_dma_start(out=a_rows[:, s, 0:RANK], out_offset=None, in_=lora_a_d,
                                             in_offset=at).then_inc(rows_in, 16)

        def root(pair):
            pool.wait_ge(eps_added, pair + 1)
            nc.gpsimd.tensor_tensor(rstd[:], var_eps[:], minus_half[:], ALU.pow).then_inc(rstd_ready, 1)

        def split_piece(i):
            at = bass.ds(i * PIECE, PIECE)
            pool.wait_ge(piece_in, 16 * (i + 1))
            nc.gpsimd.tensor_copy(ffn_hi[:, at], piece[:]).then_inc(piece_hi, 1)
            pool.wait_ge(piece_hi, i + 1)
            nc.gpsimd.tensor_tensor(ffn_lo[:, at], piece[:], ffn_hi[:, at].bitcast(F32),
                                    ALU.subtract).then_inc(piece_lo, 1)

        nc.gpsimd.memset(a_rows[:], 0.0).then_inc(zeros_set, 1)
        nc.gpsimd.memset(minus_half[:], -0.5).then_inc(zeros_set, 1)
        nc.gpsimd.memset(v_wide[:], 0.0).then_inc(zeros_set, 1)
        nc.gpsimd.memset(recip[:], 0.0).then_inc(zeros_set, 1)
        pool.wait_ge(zeros_set, 4)
        pool.wait_ge(idx_in, 16)
        gather(0)
        root(0)
        gather(1)
        root(1)
        gather(2)

        def body(i, roots=True, gathers=True):
            split_piece(i)
            if roots:
                root(i + 2)
            if gathers:
                gather(i + 3)

        body(0)
        with pool.Fori(1, PAIRS - 3) as i:
            body(i)
        body(PAIRS - 3, gathers=False)
        body(PAIRS - 2, roots=False, gathers=False)
        body(PAIRS - 1, roots=False, gathers=False)

    @block.tensor
    def _(pe):
        def turn_a(pair):
            pe.wait_ge(rows_in, 64 * (pair + 1))
            for s in range(2):
                mm = nc.tensor.transpose(attn_ps[:, D + s * P:D + (s + 1) * P], a_rows[:, s, :], ident[:])
            mm.then_inc(a_turned, 1)

        def lora(pair):
            pe.wait_ge(a_out, pair + 1)
            need(pe, turn_odd_out, 4 * (pair - 1))
            for s in range(2):
                mm = nc.tensor.matmul(turn_ps[1][:, s * D:(s + 1) * D], a_T[:, s * P:(s + 1) * P], lora_b[:],
                                      start=True, stop=True)
            mm.then_inc(lora_done, 1)

        def turn_x(pair):
            pe.wait_ge(normed, 2 * pair + 2)
            need(pe, v_out, pair)
            for s in range(2):
                for k in range(KC):
                    mm = nc.tensor.transpose(misc_ps[:, (2 * k + s) * P:(2 * k + s + 1) * P],
                                             xn[:, s, k * P:(k + 1) * P], ident[:])
            mm.then_inc(x_turned, 1)

        def project(pair, w, ps):
            for m in range(KC):
                for k in range(KC):
                    for n, (a, b) in enumerate(PASSES):
                        mm = nc.tensor.matmul(ps[:, m * D:(m + 1) * D], attn_w[:, a, w, k, m * P:(m + 1) * P],
                                              xT[:, b, k, :], start=(k == 0 and n == 0),
                                              stop=(k == KC - 1 and n == 2))
            return mm

        def project_k(pair):
            pe.wait_ge(x_hi, pair + 1)
            pe.wait_ge(x_lo, pair + 1)
            project(pair, 1, misc_ps).then_inc(k_done, 1)

        def project_q(pair):
            need(pe, turn_even_out, 4 * pair - 2)
            project(pair, 0, turn_ps[0]).then_inc(q_done, 1)

        def project_v(pair):
            pe.wait_ge(k_hi, pair + 1)
            pe.wait_ge(k_lo, pair + 1)
            for s in range(2):
                for k in range(KC):
                    for n, (a, b) in enumerate(PASSES):
                        mm = nc.tensor.matmul(misc_ps[:, s * D:(s + 1) * D], xT[:, a, k, s * P:(s + 1) * P],
                                              attn_w[:, b, 2, k, :], start=(k == 0 and n == 0),
                                              stop=(k == KC - 1 and n == 2))
            mm.then_inc(v_done, 1)

        def scores(n, s, half):
            groups = (2 * half, 2 * half + 1)
            for g in groups:
                need(pe, masked, 4 * n - 3 + g)
            for c in range(KC):
                for t, (a, b) in enumerate(PASSES):
                    for g in groups:
                        r = 32 * g
                        mm = nc.tensor.matmul(
                            scores_ps[g][:, c * 2 * P:(c + 1) * 2 * P].rearrange("p (e k) -> p e k", e=2),
                            qT[r:r + 32, a, c, s * P:(s + 1) * P], kT[r:r + 32, b, c, :, s * P:(s + 1) * P],
                            start=(t == 0), stop=(t == 2))
                        if c == KC - 1 and t == 2:
                            mm.then_inc(scores_done, 1)

        def turn_probs(n, g):
            pe.wait_ge(exps, 4 * n + g + 1)
            for j in range(4):
                mm = nc.tensor.transpose(turn_ps[g % 2][:, j * P:(j + 1) * P], probs[:, 4 * g + j, :], ident[:])
            mm.then_inc(turned, 1)

        def turn_recip(n):
            pe.wait_ge(recip_done, n + 1)
            need(pe, added, n)
            nc.tensor.transpose(attn_ps[:, D:D + P], recip[:], ident[:]).then_inc(recip_turned, 1)

        def attend(n, s):
            pe.wait_ge(recip_T_out, n + 1)
            pe.wait_ge(turn_even_out, 2 * n + 2)
            pe.wait_ge(turn_odd_out, 2 * n + 2)
            for c in range(KC):
                nc.tensor.matmul(attn_ps[:, D + c * P:D + (c + 1) * P], head_sel[:, c, :], recip_T[:],
                                 start=True, stop=True)
            for c in range(KC):
                for e in range(2):
                    for g in range(4):
                        mm = nc.tensor.matmul(attn_ps[32 * g:32 * g + 32, c * P:(c + 1) * P],
                                              v_wide[:, s, 8 * c + 2 * g + e, :], probs_T[:, slot(g, c, e), :],
                                              start=(e == 0), stop=(e == 1))
            mm.then_inc(attn_done, 1)

        def project_out(n):
            pe.wait_ge(attn_lo, n + 1)
            for c in range(KC):
                for t, (a, b) in enumerate(PASSES):
                    mm = nc.tensor.matmul(attn_ps[:, 0:D], attn_r[:, a, c * P:(c + 1) * P], attn_w[:, b, 3, c, :],
                                          start=(c == 0 and t == 0), stop=(c == KC - 1 and t == 2))
            mm.then_inc(out_done, 1)

        def qk_read(pair):
            pe.wait_ge(q_hi, pair + 1)
            pe.wait_ge(q_lo, pair + 1)
            pe.wait_ge(k_hi, pair + 1)
            pe.wait_ge(k_lo, pair + 1)

        pe.wait_ge(const_in, 64)
        pe.wait_ge(zeros_set, 4)
        turn_a(0)
        pe.wait_ge(b_scaled, 1)
        lora(0)
        turn_x(0)
        pe.wait_ge(a_out, 1)
        turn_a(1)
        pe.wait_ge(w_hi, 1)
        pe.wait_ge(w_lo, 1)
        project_k(0)
        project_q(0)
        pe.wait_ge(embedded, 2)
        lora(1)
        project_v(0)
        qk_read(0)
        scores(0, 0, 0)
        scores(0, 0, 1)

        def body(i, first=False, following=True, after=True):
            a, b, before = 2 * i, 2 * i + 1, 2 * i - 1
            need(pe, turn_even_out, 4 * i)
            turn_probs(a, 0)
            if following:
                pe.wait_ge(embedded, 2 * i + 4)
            else:
                pe.wait_ge(turn_odd_out, 4 * i)
            turn_probs(a, 1)
            if following:
                turn_x(i + 1)
            scores(b, 1, 0)
            if not first:
                project_out(before)
            if following:
                project_k(i + 1)
            pe.wait_ge(turn_even_out, 2 * a + 1)
            turn_probs(a, 2)
            pe.wait_ge(turn_odd_out, 2 * a + 1)
            turn_probs(a, 3)
            if first:
                pe.wait_ge(a_out, 2)
            turn_recip(a)
            scores(b, 1, 1)
            if following:
                project_q(i + 1)
            attend(a, 0)

            if following:
                pe.wait_ge(q_hi, i + 2)
                pe.wait_ge(q_lo, i + 2)
            else:
                pe.wait_ge(turn_even_out, 2 * a + 2)
            turn_probs(b, 0)
            pe.wait_ge(turn_odd_out, 2 * a + 2)
            turn_probs(b, 1)
            if following:
                qk_read(i + 1)
                scores(b + 1, 0, 0)
            if after:
                pe.wait_ge(attn_normed, a + 1)
                turn_a(i + 2)
            project_out(a)
            if following:
                project_v(i + 1)
            pe.wait_ge(turn_even_out, 2 * b + 1)
            turn_probs(b, 2)
            pe.wait_ge(turn_odd_out, 2 * b + 1)
            turn_probs(b, 3)
            if after:
                pe.wait_ge(a_out, i + 3)
            turn_recip(b)
            if following:
                scores(b + 1, 0, 1)
            if after:
                lora(i + 2)
            attend(b, 1)

        body(0, first=True)
        with pe.Fori(1, PAIRS - 2) as i:
            body(i)
        body(PAIRS - 2, after=False)
        body(PAIRS - 1, following=False, after=False)
        project_out(SEQS - 1)

    @block.vector
    def _(dve):
        def mask_scores(n, *groups):
            for g in groups:
                need_before(dve, w_lo, 1, (scores_done, 4 * n + g + 1), (turned, 4 * n - 3 + g))
                for j in range(4):
                    last = nc.vector.tensor_tensor_reduce(
                        probs[:, 4 * g + j, :], scores_ps[g][:, j * P:(j + 1) * P], mask[:], 1.0, NEVER,
                        ALU.add, ALU.min, neg_max[:, 4 * g + j:4 * g + j + 1])
                last.then_inc(masked, 1)

        def invert_sums(n):
            dve.wait_ge(exps, 4 * n + 4)
            need(dve, recip_turned, n)
            nc.vector.reciprocal(recip[:, 0:HEADS], sums[:]).then_inc(recip_done, 1)

        def turn_recip(n):
            dve.wait_ge(recip_turned, n + 1)
            need(dve, attn_done, n)
            nc.vector.tensor_copy(recip_T[:], attn_ps[0:HEADS, D:D + P]).then_inc(recip_T_out, 1)

        def norm_attention(n):
            dve.wait_ge(attn_done, n + 1)
            nc.vector.tensor_copy(recip_rows[:], attn_ps[:, D:2 * D]).then_inc(recip_rows_out, 1)
            dve.wait_ge(recip_rows_out, n + 1)
            nc.vector.tensor_tensor(attn[:], attn_ps[:, 0:D], recip_rows[:], ALU.mult).then_inc(attn_normed, 1)
            dve.wait_ge(attn_normed, n + 1)
            need(dve, out_done, n)
            nc.vector.tensor_copy(attn_r[:, 0, :], attn[:]).then_inc(attn_hi, 1)
            dve.wait_ge(attn_hi, n + 1)
            nc.vector.tensor_tensor(attn_r[:, 1, :], attn[:], attn_r[:, 0, :].bitcast(F32),
                                    ALU.subtract).then_inc(attn_lo, 1)

        def copy_a(pair, out_before):
            dve.wait_ge(a_turned, pair + 1)
            need(dve, out_done, out_before)
            need(dve, lora_done, pair)
            nc.vector.tensor_copy(a_T[:], attn_ps[0:RANK, D:D + 2 * P]).then_inc(a_out, 1)

        def embed(pair):
            dve.wait_ge(lora_done, pair + 1)
            dve.wait_ge(rows_in, 64 * (pair + 1))
            for s in range(2):
                n = 2 * pair + s
                nc.vector.tensor_tensor(h[:, n, :], turn_ps[1][:, s * D:(s + 1) * D], emb_rows[:, s, :],
                                        ALU.add).then_inc(embedded, 1)
            for s in range(2):
                n = 2 * pair + s
                need_before(dve, w_lo, 1, (embedded, n + 1))
                nc.vector.bn_stats(stats[:, s, :], h[:, n, :]).then_inc(stats_done, 1)
            for s in range(2):
                n = 2 * pair + s
                need_before(dve, w_lo, 1, (stats_done, n + 1))
                nc.vector.bn_aggr(mean_var[:, s, :], stats[:, s, :]).then_inc(mv_done, 1)
            dve.wait_ge(mv_done, 2 * pair + 2)
            need(dve, rstd_ready, pair)
            nc.vector.tensor_scalar(var_eps[:], mean_var[:, :, 1], EPS, None, ALU.add).then_inc(eps_added, 1)

        def norm(pair):
            dve.wait_ge(rstd_ready, pair + 1)
            need(dve, x_turned, pair)
            for s in range(2):
                n = 2 * pair + s
                nc.vector.tensor_scalar(xn[:, s, :], h[:, n, :], mean_var[:, s, 0:1], rstd[:, s:s + 1],
                                        ALU.subtract, ALU.mult).then_inc(normed, 1)

        def add_attention(n):
            dve.wait_ge(out_done, n + 1)
            nc.vector.tensor_tensor(h[:, n, :], attn_ps[:, 0:D], h[:, n, :], ALU.add).then_inc(added, 1)

        def copy_turned(n, g):
            dve.wait_ge(turned, 4 * n + g + 1)
            need(dve, attn_done, n)
            nc.vector.tensor_copy(probs_T[:, 4 * g:4 * g + 4, :],
                                  turn_ps[1][:].rearrange("p (j q) -> p j q", j=4)).then_inc(turn_odd_out, 1)

        def low_x(pair):
            dve.wait_ge(x_turned, pair + 1)
            dve.wait_ge(x_hi, pair + 1)
            need(dve, v_done, pair)
            nc.vector.tensor_tensor(xT[:, 1].rearrange("p k n -> p (k n)"), misc_ps[:],
                                    xT[:, 0].rearrange("p k n -> p (k n)").bitcast(F32),
                                    ALU.subtract).then_inc(x_lo, 1)

        def low_q(pair):
            need(dve, scores_done, 8 * pair)
            dve.wait_ge(q_hi, pair + 1)
            nc.vector.scalar_tensor_tensor(out=qT[:, 1], in0=turn_ps[0][:].rearrange("p (c n) -> p c n", c=KC),
                                           scalar=-DK ** -0.5, in1=qT[:, 0].bitcast(F32), op0=ALU.mult,
                                           op1=ALU.subtract).then_inc(q_lo, 1)

        def low_k(pair):
            need(dve, scores_done, 8 * pair)
            dve.wait_ge(k_hi, pair + 1)
            for e in range(2):
                last = nc.vector.scalar_tensor_tensor(
                    out=kT[:, 1, :, e, :], in0=misc_ps[:].rearrange("p (c n) -> p c n", c=KC),
                    scalar=parity[:, e:e + 1], in1=kT[:, 0, :, e, :].bitcast(F32), op0=ALU.mult, op1=ALU.subtract)
            last.then_inc(k_lo, 1)

        dve.wait_ge(b_in, 16)
        nc.vector.tensor_scalar(lora_b[:], lora_b[:], LORA_SCALE, None, ALU.mult).then_inc(b_scaled, 1)
        dve.wait_ge(w_hi, 1)
        nc.vector.tensor_tensor(attn_w[:, 1].rearrange("p w k n -> p (w k n)"), probs[:].rearrange("p a b -> p (a b)"),
                                attn_w[:, 0].rearrange("p w k n -> p (w k n)").bitcast(F32),
                                ALU.subtract).then_inc(w_lo, 1)
        dve.wait_ge(const_in, 64)
        dve.wait_ge(zeros_set, 4)
        dve.wait_ge(w_lo, 1)
        copy_a(0, 0)
        embed(0)
        norm(0)
        low_x(0)
        copy_a(1, 0)
        low_k(0)
        low_q(0)
        embed(1)
        norm(1)
        mask_scores(0, 0, 1, 2, 3)

        def body(i, first=False, following=True, after=True):
            a, b, before = 2 * i, 2 * i + 1, 2 * i - 1
            if not first:
                norm_attention(before)
            copy_turned(a, 1)
            if following:
                low_x(i + 1)
            mask_scores(b, 0, 1)
            if not first:
                add_attention(before)
            invert_sums(a)
            copy_turned(a, 3)
            turn_recip(a)
            mask_scores(b, 2, 3)
            if following:
                low_k(i + 1)
                low_q(i + 1)

            norm_attention(a)
            copy_turned(b, 1)
            if following:
                mask_scores(b + 1, 0, 1)
            if after:
                copy_a(i + 2, a + 1)
            add_attention(a)
            invert_sums(b)
            copy_turned(b, 3)
            turn_recip(b)
            if following:
                mask_scores(b + 1, 2)
            if after:
                embed(i + 2)
            if following:
                mask_scores(b + 1, 3)
            if after:
                norm(i + 2)

        body(0, first=True)
        with dve.Fori(1, PAIRS - 2) as i:
            body(i)
        body(PAIRS - 2, after=False)
        body(PAIRS - 1, following=False, after=False)
        norm_attention(SEQS - 1)
        add_attention(SEQS - 1)

    @block.scalar
    def _(act):
        def exponents(n, g):
            act.wait_ge(masked, 4 * n + g + 1)
            if g == 0:
                need(act, recip_done, n)
            for j in range(4 * g, 4 * g + 4):
                last = nc.scalar.activation(probs[:, j, :], probs[:, j, :], ACT.Exp, bias=neg_max[:, j:j + 1],
                                            scale=-1.0, accum_out=sums[:, j:j + 1])
            last.then_inc(exps, 1)

        def copy_turned(n, g):
            act.wait_ge(turned, 4 * n + g + 1)
            need(act, attn_done, n)
            nc.scalar.activation(probs_T[:, 4 * g:4 * g + 4, :], turn_ps[0][:].rearrange("p (j q) -> p j q", j=4),
                                 ACT.Copy).then_inc(turn_even_out, 1)

        def widen_v(pair, s):
            act.wait_ge(v_done, pair + 1)
            need(act, attn_done, 2 * pair - 1 + s)
            for e in range(2):
                last = nc.scalar.activation(
                    v_wide[:, s].rearrange("p (j e) w -> p j e w", e=2)[:, :, e, e * DK:(e + 1) * DK],
                    misc_ps[:, s * D:(s + 1) * D].rearrange("p (x e w) -> p x e w", e=2, w=DK)[:, :, e, :], ACT.Copy)
            if s == 1:
                last.then_inc(v_out, 1)

        def high_x(pair):
            act.wait_ge(x_turned, pair + 1)
            need(act, v_done, pair)
            nc.scalar.activation(xT[:, 0].rearrange("p k n -> p (k n)"), misc_ps[:], ACT.Copy).then_inc(x_hi, 1)

        def high_q(pair):
            act.wait_ge(q_done, pair + 1)
            need(act, scores_done, 8 * pair)
            nc.scalar.activation(qT[:, 0], turn_ps[0][:].rearrange("p (c n) -> p c n", c=KC), ACT.Copy,
                                 scale=-DK ** -0.5).then_inc(q_hi, 1)

        def high_k(pair):
            act.wait_ge(k_done, pair + 1)
            need(act, scores_done, 8 * pair)
            for e in range(2):
                last = nc.scalar.activation(kT[:, 0, :, e, :], misc_ps[:].rearrange("p (c n) -> p c n", c=KC),
                                            ACT.Copy, scale=parity[:, e:e + 1])
            last.then_inc(k_hi, 1)

        act.wait_ge(w_in, 16)
        nc.scalar.activation(attn_w[:, 0].rearrange("p w k n -> p (w k n)"), probs[:].rearrange("p a b -> p (a b)"),
                             ACT.Copy).then_inc(w_hi, 1)
        act.wait_ge(const_in, 64)
        act.wait_ge(zeros_set, 4)
        high_x(0)
        high_k(0)
        high_q(0)
        widen_v(0, 0)
        widen_v(0, 1)
        exponents(0, 0)
        exponents(0, 1)

        def body(i, following=True):
            a, b = 2 * i, 2 * i + 1
            copy_turned(a, 0)
            if following:
                high_x(i + 1)
            exponents(a, 2)
            exponents(a, 3)
            copy_turned(a, 2)
            exponents(b, 0)
            if following:
                high_k(i + 1)
                high_q(i + 1)
            exponents(b, 1)

            copy_turned(b, 0)
            exponents(b, 2)
            exponents(b, 3)
            copy_turned(b, 2)
            if following:
                exponents(b + 1, 0)
                widen_v(i + 1, 0)
                exponents(b + 1, 1)
                widen_v(i + 1, 1)

        body(0)
        with act.Fori(1, PAIRS - 1) as i:
            body(i)
        body(PAIRS - 1, following=False)


def expert_block(nc, ctx, h, ffn_hi, ffn_lo, ident, router_d, bias_d, sel_d, out_d):
    def sb(name, shape, dt=F32):
        return ctx.enter_context(nc.sbuf_tensor(name, shape, dt))

    def bank(name):
        return ctx.enter_context(nc.psum_tensor(name, [P, 512], F32))

    def sem(name):
        return ctx.enter_context(nc.semaphore(name))

    parts = [w[:].rearrange("p (t n) -> p t n", t=3) for w in (ffn_hi, ffn_lo)]
    gate_w = [w[:, 0, :].rearrange("p (k n) -> p k n", k=KC) for w in parts]
    up_w = [w[:, 1, :].rearrange("p (k n) -> p k n", k=KC) for w in parts]
    down_w = [w[:, 2, :].rearrange("p (c n) -> p c n", c=CH) for w in parts]

    router_raw = sb("router_raw", [P, KC, P])
    router_w = sb("router_w", [P, 2, KC, P], F32R)
    expert_sel_raw = sb("expert_sel_raw", [2 * E, CH_ROUTED, P])
    expert_sel = sb("expert_sel", [2 * E, CH_ROUTED, P], F32R)
    bias = sb("bias", [P, E])
    earlier = sb("earlier", [P, E, E])
    minus_half = sb("minus_half2", [P, GT])
    stats = sb("stats2", [P, GT, 6])
    mean_var = sb("mean_var2", [P, GT, 2])
    var_eps = sb("var_eps2", [P, GT])
    rstd = sb("rstd2", [P, GT])
    xn = sb("xn2", [P, GT, D])
    xT = sb("xT2", [P, 2, 2, KC, TOK], F32R)
    score_T = sb("score_T", [E, TOK])
    score = sb("score", [P, GT, E])
    biased = sb("biased", [P, GT, E])
    pair_sums = sb("pair_sums", [P, GT, EG, 6])
    group_score = sb("group_score", [P, GT, EG])
    beats = sb("beats", [P, 2, E, E])
    ties = sb("ties", [P, 2, E, E])
    group_rank = sb("group_rank", [P, GT, EG])
    group_on = sb("group_on", [P, GT, EG])
    group_off = sb("group_off", [P, GT, EG])
    candidates = sb("candidates", [P, GT, E])
    rank = sb("rank", [P, GT, E])
    weight = sb("weight", [P, GT, E])
    total = sb("total", [P, GT])
    total_inv = sb("total_inv", [P, GT])
    combine = sb("combine", [P, GT, E])
    combine_hi = sb("combine_hi", [P, GT, E], F32R)
    combine_r = sb("combine_r", [P, GT, P])
    combine_T = sb("combine_T", [2 * E, TOK], F32R)
    silu = sb("silu", [P, 2, TOK])
    scaled = sb("scaled", [P, 2, TOK])
    hid = sb("hid", [P, 2, TOK])
    hid_hi = sb("hid_hi", [P, 2, TOK], F32R)
    hid_lo = sb("hid_lo", [P, 2, TOK], F32R)

    gate_ps = [bank(f"gate_ps{k}") for k in range(2)]
    up_ps = [bank(f"up_ps{k}") for k in range(2)]
    combine_ps = bank("combine_ps")
    out_ps = [bank(f"out_ps{k}") for k in range(2)]
    misc_ps = bank("misc_ps2")

    const_in, stored = sem("const2_in"), sem("stored")
    zeros_set, rstd_ready = sem("zeros2_set"), sem("rstd2_ready")
    x_turned, logits_done, score_turned, combine_turned = (sem("x2_turned"), sem("logits_done"), sem("score_turned"),
                                                           sem("combine_turned"))
    gate_done, up_done, spread_done, down_done = sem("gate_done"), sem("up_done"), sem("spread_done"), sem("down_done")
    router_lo, eps_added, normed, x_lo = sem("router_lo"), sem("eps2_added"), sem("normed2"), sem("x2_lo")
    combine_hi_done = sem("combine_hi_done")
    step, score_out, combined, scaled_done = sem("step"), sem("score_out"), sem("combined"), sem("scaled_done")
    hid_done, hid_lo_done, y_done = sem("hid_done"), sem("hid_lo_done"), sem("y_done")
    consts_cast, x_hi, scored, combine_T_out = sem("consts_cast"), sem("x2_hi"), sem("scored"), sem("combine_T_out")
    silu_done, hid_hi_done = sem("silu_done"), sem("hid_hi_done")

    block = ctx.enter_context(nc.Block())
    out_rows = out_d.rearrange("(t p) d -> p t d", p=P)


    @block.sync
    def _(sp):
        sp.dma_start(router_raw[:], router_d).then_inc(const_in, 16)
        sp.dma_start(expert_sel_raw[:], sel_d).then_inc(const_in, 16)
        sp.dma_start(bias[:], bias_d).then_inc(const_in, 16)

        with sp.Fori(0, GROUPS) as g:
            sp.wait_ge(y_done, 2 * g + 2)
            sp.dma_start(out_rows[:, bass.ds(GT * g, GT), :], h[:, bass.ds(GT * g, GT), :]).then_inc(stored, 16)
        sp.wait_ge(stored, 16 * GROUPS)

    @block.gpsimd
    def _(pool):
        nc.gpsimd.memset(combine_r[:], 0.0).then_inc(zeros_set, 1)
        nc.gpsimd.memset(minus_half[:], -0.5).then_inc(zeros_set, 1)
        nc.gpsimd.memset(earlier[:], 1.0).then_inc(zeros_set, 1)
        pool.wait_ge(zeros_set, 3)
        nc.gpsimd.affine_select(out=earlier[:], in_=earlier[:], compare_op=ALU.is_gt, fill=0.0, base=0,
                                pattern=[[1, E], [-1, E]], channel_multiplier=0).then_inc(zeros_set, 1)

        def root(g):
            pool.wait_ge(eps_added, g + 1)
            nc.gpsimd.tensor_tensor(rstd[:], var_eps[:], minus_half[:], ALU.pow).then_inc(rstd_ready, 1)

        with pool.Fori(0, GROUPS) as g:
            root(g)

    @block.tensor
    def _(pe):
        def turn_x(g, k):
            pe.wait_ge(normed, g + 1)
            if k == 0:
                need(pe, combine_T_out, g)
            else:
                pe.wait_ge(x_hi, 2 * g + 1)
                pe.wait_ge(x_lo, 2 * g + 1)
            for t in range(GT):
                mm = nc.tensor.transpose(misc_ps[:, t * P:(t + 1) * P], xn[:, t, k * P:(k + 1) * P], ident[:])
            mm.then_inc(x_turned, 1)

        def logits(g, parity):
            pe.wait_ge(x_hi, 2 * g + 2)
            pe.wait_ge(x_lo, 2 * g + 2)
            for k in range(KC):
                for n, (a, b) in enumerate(PASSES):
                    mm = nc.tensor.matmul(misc_ps[:], router_w[:, a, k, :], xT[:, parity, b, k, :],
                                          start=(k == 0 and n == 0), stop=(k == KC - 1 and n == 2))
            mm.then_inc(logits_done, 1)

        def turn_scores(g):
            need_before(pe, zeros_set, 4, (scored, g + 1))
            for t in range(GT):
                mm = nc.tensor.transpose(misc_ps[:, t * E:(t + 1) * E], score_T[:, t * P:(t + 1) * P],
                                         ident[0:E, 0:E])
            mm.then_inc(score_turned, 1)

        def turn_combine(g):
            pe.wait_ge(combined, g + 1)
            pe.wait_ge(score_out, g + 1)
            for t in range(GT):
                mm = nc.tensor.transpose(misc_ps[:, t * P:(t + 1) * P], combine_r[:, t, :], ident[:])
            mm.then_inc(combine_turned, 1)

        def spread(g, c):
            if c == 0:
                pe.wait_ge(combine_T_out, g + 1)
            need(pe, scaled_done, CH_ROUTED * g + c)
            nc.tensor.matmul(combine_ps[:], expert_sel[:, c, :], combine_T[:], start=True,
                             stop=True).then_inc(spread_done, 1)

        def up_or_gate(g, parity, c, w, ps):
            for k in range(KC):
                for n, (a, b) in enumerate(PASSES):
                    mm = nc.tensor.matmul(ps[:], w[a][:, k, c * P:(c + 1) * P], xT[:, parity, b, k, :],
                                          start=(k == 0 and n == 0), stop=(k == KC - 1 and n == 2))
            return mm

        def down(g, c):
            pe.wait_ge(hid_hi_done, CH * g + c + 1)
            pe.wait_ge(hid_lo_done, CH * g + c + 1)
            hid_r = (hid_hi, hid_lo)
            for t in range(GT):
                if c == 0 and t % 2 == 0:
                    need(pe, y_done, 2 * g - 1 + t // 2)
                for n, (a, b) in enumerate(PASSES):
                    mm = nc.tensor.matmul(out_ps[t // 2][:, (t % 2) * D:(t % 2 + 1) * D],
                                          hid_r[a][:, c % 2, t * P:(t + 1) * P], down_w[b][:, c, :],
                                          start=(c == 0 and n == 0 and t % 2 == 0),
                                          stop=(c == CH - 1 and n == 2), skip_group_check=True)
            mm.then_inc(down_done, 1)

        def experts(g, parity, first=False, route=True):
            for c in range(CH):
                if c < CH_ROUTED:
                    spread(g, c)
                need(pe, silu_done, CH * g + c - 1)
                up_or_gate(g, parity, c, gate_w, gate_ps[c % 2]).then_inc(gate_done, 1)
                need(pe, hid_done, CH * g + c - 1)
                up_or_gate(g, parity, c, up_w, up_ps[c % 2]).then_inc(up_done, 1)
                if route and c in (2, 4):
                    turn_x(g + 1, (c - 2) // 2)
                if route and c == 6:
                    logits(g + 1, 1 - parity)
                if route and c == 8:
                    turn_scores(g + 1)
                if route and c == 11:
                    turn_combine(g + 1)
                if c > 0:
                    down(g, c - 1)
                elif not first:
                    down(g - 1, CH - 1)

        pe.wait_ge(consts_cast, 2)
        pe.wait_ge(router_lo, 1)
        pe.wait_ge(zeros_set, 4)
        turn_x(0, 0)
        turn_x(0, 1)
        logits(0, 0)
        turn_scores(0)
        turn_combine(0)
        experts(0, 0, first=True)
        with pe.Fori(0, GROUPS // 2 - 1) as j:
            experts(2 * j + 1, 1)
            experts(2 * j + 2, 0)
        experts(GROUPS - 1, 1, route=False)
        down(GROUPS - 1, CH - 1)

    @block.vector
    def _(dve):
        STEPS = 26

        def norm_rows(g):
            for t in range(GT):
                last = nc.vector.bn_stats(stats[:, t, :], h[:, GT * g + t, :])
            last.then_inc(step, 1)
            need_before(dve, zeros_set, 4, (step, STEPS * g + 1))
            for t in range(GT):
                last = nc.vector.bn_aggr(mean_var[:, t, :], stats[:, t, :])
            last.then_inc(step, 1)
            dve.wait_ge(step, STEPS * g + 2)
            nc.vector.tensor_scalar(var_eps[:], mean_var[:, :, 1], EPS, None, ALU.add).then_inc(eps_added, 1)
            dve.wait_ge(rstd_ready, g + 1)
            need(dve, x_turned, 2 * g)
            for t in range(GT):
                last = nc.vector.tensor_scalar(xn[:, t, :], h[:, GT * g + t, :], mean_var[:, t, 0:1],
                                               rstd[:, t:t + 1], ALU.subtract, ALU.mult)
            last.then_inc(normed, 1)

        def low_x(g, parity, k):
            dve.wait_ge(x_turned, 2 * g + k + 1)
            dve.wait_ge(x_hi, 2 * g + k + 1)
            nc.vector.tensor_tensor(xT[:, parity, 1, k, :], misc_ps[:], xT[:, parity, 0, k, :].bitcast(F32),
                                    ALU.subtract).then_inc(x_lo, 1)

        def route(g):
            done = [2]

            def then(last):
                done[0] += 1
                last.then_inc(step, 1)
                dve.wait_ge(step, STEPS * g + done[0])

            tt = nc.vector.tensor_tensor
            dve.wait_ge(score_turned, g + 1)
            nc.vector.tensor_copy(score[:], misc_ps[:, 0:GT * E].rearrange("p (t e) -> p t e", t=GT)
                                  ).then_inc(score_out, 1)
            dve.wait_ge(score_out, g + 1)
            then(tt(biased[:], score[:], bias[:].unsqueeze(1).to_broadcast([P, GT, E]), ALU.add))
            b4 = biased[:].rearrange("p t (g i) -> p t g i", g=EG)
            at = 0
            for d in (1, 2, 3):
                last = tt(pair_sums[:, :, :, at:at + 4 - d], b4[:, :, :, 0:4 - d], b4[:, :, :, d:4], ALU.add)
                at += 4 - d
            then(last)
            then(nc.vector.tensor_reduce(group_score[:], pair_sums[:], AX_X, ALU.max))
            gs = group_score[:]
            gi = gs.unsqueeze(3).to_broadcast([P, GT, EG, EG])
            gj = gs.unsqueeze(2).to_broadcast([P, GT, EG, EG])
            more = beats[:, 0, 0:GT, :].rearrange("p t (i j) -> p t i j", i=EG)
            same = ties[:, 0, 0:GT, :].rearrange("p t (i j) -> p t i j", i=EG)
            early = earlier[:, 0:EG, 0:EG].unsqueeze(1).to_broadcast([P, GT, EG, EG])
            tt(more, gj, gi, ALU.is_gt)
            then(tt(same, gj, gi, ALU.is_equal))
            then(tt(same, same, early, ALU.mult))
            then(tt(more, more, same, ALU.add))
            then(nc.vector.tensor_reduce(group_rank[:], more, AX_X, ALU.add))
            nc.vector.tensor_scalar(group_on[:], group_rank[:], 1.5, None, ALU.is_lt)
            then(nc.vector.tensor_scalar(group_off[:], group_rank[:], 1.5, -NEVER, ALU.is_gt, ALU.mult))
            c4 = candidates[:].rearrange("p t (g i) -> p t g i", g=EG)
            then(tt(c4, b4, group_on[:].unsqueeze(3).to_broadcast([P, GT, EG, 4]), ALU.mult))
            then(tt(c4, c4, group_off[:].unsqueeze(3).to_broadcast([P, GT, EG, 4]), ALU.add))
            early = earlier[:].unsqueeze(1).to_broadcast([P, 2, E, E])
            for half in range(2):
                cs = candidates[:, 2 * half:2 * half + 2, :]
                ci = cs.unsqueeze(3).to_broadcast([P, 2, E, E])
                cj = cs.unsqueeze(2).to_broadcast([P, 2, E, E])
                tt(beats[:], cj, ci, ALU.is_gt)
                then(tt(ties[:], cj, ci, ALU.is_equal))
                then(tt(ties[:], ties[:], early, ALU.mult))
                then(tt(beats[:], beats[:], ties[:], ALU.add))
                then(nc.vector.tensor_reduce(rank[:, 2 * half:2 * half + 2, :], beats[:], AX_X, ALU.add))
            then(nc.vector.tensor_scalar(rank[:], rank[:], 3.5, None, ALU.is_lt))
            then(tt(weight[:], score[:], rank[:], ALU.mult))
            then(nc.vector.tensor_reduce(total[:], weight[:], AX_X, ALU.add))
            then(nc.vector.tensor_scalar(total[:], total[:], 1e-20, None, ALU.add))
            then(nc.vector.reciprocal(total_inv[:], total[:]))
            need(dve, combine_turned, g)
            then(tt(combine[:], weight[:], total_inv[:].unsqueeze(2).to_broadcast([P, GT, E]), ALU.mult))
            assert done[0] == STEPS, done
            return tt

        def split_combine(g):
            nc.vector.tensor_copy(combine_hi[:], combine[:]).then_inc(combine_hi_done, 1)
            dve.wait_ge(combine_hi_done, g + 1)
            nc.vector.tensor_copy(combine_r[:, :, 0:E], combine_hi[:].bitcast(F32))
            nc.vector.tensor_tensor(combine_r[:, :, E:2 * E], combine[:], combine_hi[:].bitcast(F32),
                                    ALU.subtract).then_inc(combined, 1)

        def hidden(g, c):
            dve.wait_ge(silu_done, CH * g + c + 1)
            n = CH * g + c
            if c < CH_ROUTED:
                dve.wait_ge(spread_done, CH_ROUTED * g + c + 1)
                nc.vector.tensor_tensor(scaled[:, c % 2, :], combine_ps[:], silu[:, c % 2, :],
                                        ALU.mult).then_inc(scaled_done, 1)
                dve.wait_ge(scaled_done, CH_ROUTED * g + c + 1)
                left = scaled
            else:
                left = silu
            dve.wait_ge(up_done, n + 1)
            need(dve, hid_hi_done, n - 1)
            nc.vector.tensor_tensor(hid[:, c % 2, :], up_ps[c % 2][:], left[:, c % 2, :], ALU.mult
                                    ).then_inc(hid_done, 1)
            dve.wait_ge(hid_done, n + 1)
            dve.wait_ge(hid_hi_done, n + 1)
            nc.vector.tensor_tensor(hid_lo[:, c % 2, :], hid[:, c % 2, :], hid_hi[:, c % 2, :].bitcast(F32),
                                    ALU.subtract).then_inc(hid_lo_done, 1)

        def finish(g):
            dve.wait_ge(down_done, CH * g + CH)
            for k in range(2):
                rows = h[:, bass.ds(GT * g + 2 * k, 2), :]
                nc.vector.tensor_tensor(rows, out_ps[k][:].rearrange("p (t d) -> p t d", t=2), rows,
                                        ALU.add).then_inc(y_done, 1)

        def experts(g, parity, first=False, routes=True):
            for c in range(CH):
                if routes and c == 0:
                    norm_rows(g + 1)
                hidden(g, c)
                if c == 0 and not first:
                    finish(g - 1)
                if routes and c in (2, 4):
                    low_x(g + 1, 1 - parity, (c - 2) // 2)
                if routes and c == 8:
                    route(g + 1)
                    split_combine(g + 1)

        dve.wait_ge(const_in, 48)
        dve.wait_ge(zeros_set, 4)
        dve.wait_ge(consts_cast, 2)
        nc.vector.tensor_tensor(router_w[:, 1], router_raw[:], router_w[:, 0].bitcast(F32),
                                ALU.subtract).then_inc(router_lo, 1)
        norm_rows(0)
        low_x(0, 0, 0)
        low_x(0, 0, 1)
        route(0)
        split_combine(0)
        experts(0, 0, first=True)
        with dve.Fori(0, GROUPS // 2 - 1) as j:
            experts(2 * j + 1, 1)
            experts(2 * j + 2, 0)
        experts(GROUPS - 1, 1, routes=False)
        finish(GROUPS - 1)

    @block.scalar
    def _(act):
        def high_x(g, parity, k):
            act.wait_ge(x_turned, 2 * g + k + 1)
            need(act, up_done, CH * (g - 1))
            nc.scalar.activation(xT[:, parity, 0, k, :], misc_ps[:], ACT.Copy).then_inc(x_hi, 1)

        def score_rows(g):
            act.wait_ge(logits_done, g + 1)
            nc.scalar.activation(score_T[:], misc_ps[0:E, :], ACT.Sigmoid).then_inc(scored, 1)

        def copy_combine(g):
            act.wait_ge(combine_turned, g + 1)
            need(act, spread_done, CH_ROUTED * g)
            nc.scalar.activation(combine_T[:], misc_ps[0:2 * E, :], ACT.Copy).then_inc(combine_T_out, 1)

        def gated(g, c):
            act.wait_ge(gate_done, CH * g + c + 1)
            need(act, hid_done, CH * g + c - 1)
            nc.scalar.activation(silu[:, c % 2, :], gate_ps[c % 2][:], ACT.Silu).then_inc(silu_done, 1)

        def high_hidden(g, c):
            act.wait_ge(hid_done, CH * g + c + 1)
            need(act, down_done, CH * g + c - 1)
            nc.scalar.activation(hid_hi[:, c % 2, :], hid[:, c % 2, :], ACT.Copy).then_inc(hid_hi_done, 1)

        def experts(g, parity, routes=True):
            for c in range(CH):
                gated(g, c)
                high_hidden(g, c)
                if routes and c in (2, 4):
                    high_x(g + 1, 1 - parity, (c - 2) // 2)
                if routes and c == 6:
                    score_rows(g + 1)
                if routes and c == 11:
                    copy_combine(g + 1)

        act.wait_ge(const_in, 48)
        nc.scalar.activation(router_w[:, 0], router_raw[:], ACT.Copy).then_inc(consts_cast, 1)
        nc.scalar.activation(expert_sel[:], expert_sel_raw[:], ACT.Copy).then_inc(consts_cast, 1)
        high_x(0, 0, 0)
        high_x(0, 0, 1)
        score_rows(0)
        copy_combine(0)
        experts(0, 0)
        with act.Fori(0, GROUPS // 2 - 1) as j:
            experts(2 * j + 1, 1)
            experts(2 * j + 2, 0)
        experts(GROUPS - 1, 1, routes=False)




def kernel(x, L0_tok_W, L0_tok_A, L0_tok_B, L0_attn_q_heads, L0_attn_k_heads, L0_attn_v_heads, L0_attn_output_proj,
           L0_ffn_router_w, L0_ffn_correction_bias, L0_ffn_gate_w, L0_ffn_up_w, L0_ffn_down_w, L0_ffn_shared_gate_w,
           L0_ffn_shared_up_w, L0_ffn_shared_down_w):
    from concourse import bacc
    from concourse.bass_utils import run_bass_kernel_spmd

    def chunked(w):
        return np.concatenate(np.split(w, w.shape[0] // P), axis=1)

    attn_w = [chunked(np.asarray(w).T) for w in (L0_attn_q_heads, L0_attn_k_heads, L0_attn_v_heads,
                                                 L0_attn_output_proj)]

    def by_channel(w, shared):
        return chunked(np.concatenate([np.asarray(w).transpose(1, 0, 2).reshape(D, -1), np.asarray(shared).T], axis=1))

    down = np.concatenate([np.asarray(L0_ffn_down_w).reshape(-1, D), np.asarray(L0_ffn_shared_down_w).T], axis=0)
    ffn_w = np.concatenate([by_channel(L0_ffn_gate_w, L0_ffn_shared_gate_w),
                            by_channel(L0_ffn_up_w, L0_ffn_shared_up_w), chunked(down)], axis=1)
    router = np.zeros((KC, P, P), np.float32)
    router[:, :, 0:E] = np.asarray(L0_ffn_router_w).T.reshape(KC, P, E)

    const = np.zeros((P, P + 2 + KC * P), np.float32)
    rows, cols = np.indices((P, P))
    const[:, 0:P] = np.where(cols > rows, np.float32(NEVER), np.float32(0))
    odd = np.arange(P) // DK % 2
    const[:, P] = odd == 0
    const[:, P + 1] = odd == 1
    for c in range(KC):
        for r in range(P):
            const[slot(r // 32, c, r // DK % 2), P + 2 + c * P + r] = 1
    sel = np.zeros((2 * E, CH_ROUTED, P), np.float32)
    for c in range(CH_ROUTED):
        for m in range(P):
            sel[2 * c + m // 64, c, m] = 1
            sel[E + 2 * c + m // 64, c, m] = 1

    arrays = {
        "idx": np.ascontiguousarray(np.asarray(x).T),
        "emb": np.ascontiguousarray(L0_tok_W),
        "lora_a": np.ascontiguousarray(L0_tok_A),
        "lora_b": np.ascontiguousarray(L0_tok_B),
        "attn_w": np.ascontiguousarray(np.concatenate(attn_w, axis=1)),
        "ffn_w": np.ascontiguousarray(ffn_w),
        "router": np.ascontiguousarray(router.transpose(1, 0, 2)),
        "bias": np.ascontiguousarray(np.broadcast_to(np.asarray(L0_ffn_correction_bias), (P, E))),
        "ident": np.eye(P, dtype=np.float32),
        "const": const,
        "sel": sel,
    }
    nc = bacc.Bacc("TRN2", target_bir_lowering=False, num_devices=1)
    args = [nc.dram_tensor(f"in_{name}", a.shape, mybir.dt.from_np(a.dtype), kind="ExternalInput").ap()
            for name, a in arrays.items()]
    out = nc.dram_tensor("out", (SEQS * P, D), F32, kind="ExternalOutput").ap()
    build(nc, *args, out)
    r = run_bass_kernel_spmd(nc, [{f"in_{name}": a for name, a in arrays.items()}], core_ids=[0])
    return r.results[0]["out"].reshape(SEQS, P, D)
```

```python
from contextlib import ExitStack

import numpy as np

import concourse.bass as bass
from concourse import mybir

ALU = mybir.AluOpType
ACT = mybir.ActivationFunctionType
AX_X = mybir.AxisListType.X
F32 = mybir.dt.float32
F32R = mybir.dt.float32r
I32 = mybir.dt.int32

P = 128
SEQS = 64
PAIRS = SEQS // 2
D = 256
KC = D // P
HEADS = 16
DK = D // HEADS
RANK = 16
LORA_SCALE = 2.0
EPS = 1e-5
E = 16
EG = 4
HID = 16 * 64 + 512
CH = HID // P
CH_ROUTED = 16 * 64 // P
CHUNKS = tuple(range(CH_ROUTED, CH)) + tuple(range(CH_ROUTED))
SHARED = CH - CH_ROUTED
STEADY = dict(normed=1, turned=(2, 3), logits=4, scores=5, candidates=6, ranked=(7, 8, 9, 10), weighed=11)
START = dict(normed=3, turned=(4, 5), logits=6, scores=7, candidates=8, ranked=(8, 9, 10, 11), weighed=11)
OWN_WEIGHED = 2
GT = 4
GROUPS = SEQS // GT
TOK = GT * P
NEVER = 3.0e38
W_COLS = 3 * CH * D
PIECE = W_COLS // PAIRS

PASSES = ((0, 0), (0, 1), (1, 0))


def need(eng, sem, count):
    if not isinstance(count, int) or count > 0:
        eng.wait_ge(sem, count)


def need_before(eng, met, met_count, *counts):
    counts = [(sem, n if isinstance(n, int) else eng.compute_val(n)) for sem, n in counts]
    eng.wait_ge(met, met_count)
    for sem, n in counts:
        need(eng, sem, n)


def slot(g, c, e):
    return 4 * g + 2 * c + e


def build(nc, idx_d, emb_d, lora_a_d, lora_b_d, attn_w_d, ffn_w_d, router_d, bias_d, ident_d, const_d, sel_d, out_d):
    with ExitStack() as whole:
        def keep(name, shape, dt=F32):
            return whole.enter_context(nc.sbuf_tensor(name, shape, dt))

        h = keep("h", [P, SEQS, D])
        ffn_hi = keep("ffn_hi", [P, W_COLS], F32R)
        ffn_lo = keep("ffn_lo", [P, W_COLS], F32R)
        ident = keep("ident", [P, P])

        with ExitStack() as ctx:
            attention_block(nc, ctx, h, ffn_hi, ffn_lo, ident, idx_d, emb_d, lora_a_d, lora_b_d, attn_w_d, ffn_w_d,
                            ident_d, const_d)
        with ExitStack() as ctx:
            expert_block(nc, ctx, h, ffn_hi, ffn_lo, ident, router_d, bias_d, sel_d, out_d)


def attention_block(nc, ctx, h, ffn_hi, ffn_lo, ident, idx_d, emb_d, lora_a_d, lora_b_d, attn_w_d, ffn_w_d,
                    ident_d, const_d):
    def sb(name, shape, dt=F32):
        return ctx.enter_context(nc.sbuf_tensor(name, shape, dt))

    def bank(name):
        return ctx.enter_context(nc.psum_tensor(name, [P, 512], F32))

    def sem(name):
        return ctx.enter_context(nc.semaphore(name))

    mask = sb("mask", [P, P])
    parity = sb("parity", [P, 2])
    head_sel = sb("head_sel", [HEADS, KC, P])
    idx = sb("idx", [P, SEQS], I32)
    lora_b = sb("lora_b", [P, 2, D], F32R)
    attn_w = sb("attn_w", [P, 2, 4, KC, D], F32R)
    piece = sb("piece", [P, PIECE])
    minus_half = sb("minus_half", [P, 2])
    idx_pair = sb("idx_pair", [P, 2], I32)
    emb_rows = sb("emb_rows", [P, 2, D])
    a_rows = sb("a_rows", [P, 2, P])
    a_T = sb("a_T", [P, 2, 2 * P], F32R)
    stats = sb("stats", [P, 2, 6])
    mean_var = sb("mean_var", [P, 2, 2])
    var_eps = sb("var_eps", [P, 2])
    rstd = sb("rstd", [P, 2])
    xn = sb("xn", [P, 2, D])
    xT = sb("xT", [P, 2, KC, 2 * P], F32R)
    qT = sb("qT", [P, 2, KC, 2 * P], F32R)
    kT = sb("kT", [P, 2, KC, 2, 2 * P], F32R)
    v_wide = sb("v_wide", [P, 2, HEADS, 2 * DK])
    probs = sb("probs", [P, HEADS, P])
    neg_max = sb("neg_max", [P, HEADS])
    sums = sb("sums", [P, HEADS])
    recip = sb("recip", [P, P])
    recip_T = sb("recip_T", [HEADS, P])
    recip_rows = sb("recip_rows", [P, KC * P])
    probs_T = sb("probs_T", [P, HEADS, P])
    attn = sb("attn", [P, KC * P])
    attn_r = sb("attn_r", [P, 2, KC * P], F32R)

    scores_ps = [bank(f"scores_ps{g}") for g in range(4)]
    turn_ps = [bank(f"turn_ps{k}") for k in range(2)]
    attn_ps = bank("attn_ps")
    misc_ps = bank("misc_ps")

    const_in, b_in, w_in, idx_in = sem("const_in"), sem("b_in"), sem("w_in"), sem("idx_in")
    rows_in, piece_in = sem("rows_in"), sem("piece_in")
    zeros_set, b_scaled, w_hi, w_lo = sem("zeros_set"), sem("b_scaled"), sem("w_hi"), sem("w_lo")
    idx_copied, rstd_ready, piece_hi, piece_lo = sem("idx_copied"), sem("rstd_ready"), sem("piece_hi"), sem("piece_lo")
    scores_done, turned, recip_turned, attn_done = sem("scores_done"), sem("turned"), sem("recip_turned"), sem("attn_done")
    a_turned, lora_done, v_done, x_turned = sem("a_turned"), sem("lora_done"), sem("v_done"), sem("x_turned")
    q_done, k_done, out_done = sem("q_done"), sem("k_done"), sem("out_done")
    masked, turn_odd_out, recip_done, recip_T_out = sem("masked"), sem("turn_odd_out"), sem("recip_done"), sem("recip_T_out")
    recip_rows_out, attn_normed, attn_hi, attn_lo = sem("recip_rows_out"), sem("attn_normed"), sem("attn_hi"), sem("attn_lo")
    a_out, embedded, stats_done, mv_done = sem("a_out"), sem("embedded"), sem("stats_done"), sem("mv_done")
    eps_added, normed, x_lo, q_lo, k_lo, added = (sem("eps_added"), sem("normed"), sem("x_lo"), sem("q_lo"),
                                                  sem("k_lo"), sem("added"))
    a_hi = sem("a_hi")
    exps, turn_even_out, v_out, x_hi, q_hi, k_hi = (sem("exps"), sem("turn_even_out"), sem("v_out"), sem("x_hi"),
                                                    sem("q_hi"), sem("k_hi"))

    block = ctx.enter_context(nc.Block())

    @block.sync
    def _(sp):
        sp.dma_start(idx[:], idx_d).then_inc(idx_in, 16)
        sp.dma_start(ident[:], ident_d).then_inc(const_in, 16)
        sp.dma_start(probs[:].rearrange("p a b -> p (a b)"), attn_w_d).then_inc(w_in, 16)
        sp.wait_ge(zeros_set, 1)
        sp.dma_start(xn[0:RANK, 0, :], lora_b_d).then_inc(b_in, 16)
        sp.dma_start(mask[:], const_d[:, 0:P]).then_inc(const_in, 16)
        sp.dma_start(parity[:], const_d[:, P:P + 2]).then_inc(const_in, 16)
        sp.dma_start(head_sel[:], const_d[0:HEADS, P + 2:P + 2 + KC * P].rearrange("h (c m) -> h c m", c=KC)
                     ).then_inc(const_in, 16)
        sp.dma_start(piece[:], ffn_w_d[:, 0:PIECE]).then_inc(piece_in, 16)
        with sp.Fori(1, PAIRS) as i:
            sp.wait_ge(piece_lo, i)
            sp.dma_start(piece[:], ffn_w_d[:, bass.ds(i * PIECE, PIECE)]).then_inc(piece_in, 16)

    @block.gpsimd
    def _(pool):
        def gather(pair):
            need(pool, embedded, 2 * pair)
            nc.gpsimd.tensor_copy(idx_pair[:], idx[:, bass.ds(2 * pair, 2)]).then_inc(idx_copied, 1)
            need_before(pool, idx_in, 16, (idx_copied, pair + 1))
            for s in range(2):
                at = bass.IndirectOffsetOnAxis(ap=idx_pair[:, s:s + 1], axis=0)
                nc.gpsimd.indirect_dma_start(out=emb_rows[:, s, :], out_offset=None, in_=emb_d,
                                             in_offset=at).then_inc(rows_in, 16)
                nc.gpsimd.indirect_dma_start(out=a_rows[:, s, 0:RANK], out_offset=None, in_=lora_a_d,
                                             in_offset=at).then_inc(rows_in, 16)

        def root(pair):
            pool.wait_ge(eps_added, pair + 1)
            nc.gpsimd.tensor_tensor(rstd[:], var_eps[:], minus_half[:], ALU.pow).then_inc(rstd_ready, 1)

        def split_piece(i):
            at = bass.ds(i * PIECE, PIECE)
            pool.wait_ge(piece_in, 16 * (i + 1))
            nc.gpsimd.tensor_copy(ffn_hi[:, at], piece[:]).then_inc(piece_hi, 1)
            pool.wait_ge(piece_hi, i + 1)
            nc.gpsimd.tensor_tensor(ffn_lo[:, at], piece[:], ffn_hi[:, at].bitcast(F32),
                                    ALU.subtract).then_inc(piece_lo, 1)

        nc.gpsimd.memset(xn[:, 0, :], 0.0).then_inc(zeros_set, 1)
        nc.gpsimd.memset(a_rows[:], 0.0).then_inc(zeros_set, 1)
        nc.gpsimd.memset(minus_half[:], -0.5).then_inc(zeros_set, 1)
        nc.gpsimd.memset(v_wide[:], 0.0).then_inc(zeros_set, 1)
        nc.gpsimd.memset(recip[:], 0.0).then_inc(zeros_set, 1)
        pool.wait_ge(zeros_set, 5)
        pool.wait_ge(idx_in, 16)
        gather(0)
        root(0)
        gather(1)
        root(1)
        gather(2)

        def body(i, roots=True, gathers=True):
            split_piece(i)
            if roots:
                root(i + 2)
            if gathers:
                gather(i + 3)

        body(0)
        with pool.Fori(1, PAIRS - 3) as i:
            body(i)
        body(PAIRS - 3, gathers=False)
        body(PAIRS - 2, roots=False, gathers=False)
        body(PAIRS - 1, roots=False, gathers=False)

    @block.tensor
    def _(pe):
        def turn_a(pair):
            pe.wait_ge(rows_in, 64 * (pair + 1))
            for s in range(2):
                mm = nc.tensor.transpose(attn_ps[:, D + s * P:D + (s + 1) * P], a_rows[:, s, :], ident[:])
            mm.then_inc(a_turned, 1)

        def lora(pair):
            pe.wait_ge(a_out, pair + 1)
            need(pe, turn_odd_out, 4 * (pair - 1))
            for s in range(2):
                for n, (a, b) in enumerate(PASSES):
                    mm = nc.tensor.matmul(turn_ps[1][:, s * D:(s + 1) * D], a_T[:, a, s * P:(s + 1) * P],
                                          lora_b[:, b], start=(n == 0), stop=(n == 2))
            mm.then_inc(lora_done, 1)

        def turn_x(pair):
            pe.wait_ge(normed, 2 * pair + 2)
            need(pe, v_out, pair)
            for s in range(2):
                for k in range(KC):
                    mm = nc.tensor.transpose(misc_ps[:, (2 * k + s) * P:(2 * k + s + 1) * P],
                                             xn[:, s, k * P:(k + 1) * P], ident[:])
            mm.then_inc(x_turned, 1)

        def project(pair, w, ps):
            for m in range(KC):
                for k in range(KC):
                    for n, (a, b) in enumerate(PASSES):
                        mm = nc.tensor.matmul(ps[:, m * D:(m + 1) * D], attn_w[:, a, w, k, m * P:(m + 1) * P],
                                              xT[:, b, k, :], start=(k == 0 and n == 0),
                                              stop=(k == KC - 1 and n == 2))
            return mm

        def project_k(pair):
            pe.wait_ge(x_hi, pair + 1)
            pe.wait_ge(x_lo, pair + 1)
            project(pair, 1, misc_ps).then_inc(k_done, 1)

        def project_q(pair):
            need(pe, turn_even_out, 4 * pair - 2)
            project(pair, 0, turn_ps[0]).then_inc(q_done, 1)

        def project_v(pair):
            pe.wait_ge(k_hi, pair + 1)
            pe.wait_ge(k_lo, pair + 1)
            for s in range(2):
                for k in range(KC):
                    for n, (a, b) in enumerate(PASSES):
                        mm = nc.tensor.matmul(misc_ps[:, s * D:(s + 1) * D], xT[:, a, k, s * P:(s + 1) * P],
                                              attn_w[:, b, 2, k, :], start=(k == 0 and n == 0),
                                              stop=(k == KC - 1 and n == 2))
            mm.then_inc(v_done, 1)

        def scores(n, s, half):
            groups = (2 * half, 2 * half + 1)
            for g in groups:
                need(pe, masked, 4 * n - 3 + g)
            for c in range(KC):
                for t, (a, b) in enumerate(PASSES):
                    for g in groups:
                        r = 32 * g
                        mm = nc.tensor.matmul(
                            scores_ps[g][:, c * 2 * P:(c + 1) * 2 * P].rearrange("p (e k) -> p e k", e=2),
                            qT[r:r + 32, a, c, s * P:(s + 1) * P], kT[r:r + 32, b, c, :, s * P:(s + 1) * P],
                            start=(t == 0), stop=(t == 2))
                        if c == KC - 1 and t == 2:
                            mm.then_inc(scores_done, 1)

        def turn_probs(n, g):
            pe.wait_ge(exps, 4 * n + g + 1)
            for j in range(4):
                mm = nc.tensor.transpose(turn_ps[g % 2][:, j * P:(j + 1) * P], probs[:, 4 * g + j, :], ident[:])
            mm.then_inc(turned, 1)

        def turn_recip(n):
            pe.wait_ge(recip_done, n + 1)
            need(pe, added, n)
            nc.tensor.transpose(attn_ps[:, D:D + P], recip[:], ident[:]).then_inc(recip_turned, 1)

        def attend(n, s):
            pe.wait_ge(recip_T_out, n + 1)
            pe.wait_ge(turn_even_out, 2 * n + 2)
            pe.wait_ge(turn_odd_out, 2 * n + 2)
            for c in range(KC):
                nc.tensor.matmul(attn_ps[:, D + c * P:D + (c + 1) * P], head_sel[:, c, :], recip_T[:],
                                 start=True, stop=True)
            for c in range(KC):
                for e in range(2):
                    for g in range(4):
                        mm = nc.tensor.matmul(attn_ps[32 * g:32 * g + 32, c * P:(c + 1) * P],
                                              v_wide[:, s, 8 * c + 2 * g + e, :], probs_T[:, slot(g, c, e), :],
                                              start=(e == 0), stop=(e == 1))
            mm.then_inc(attn_done, 1)

        def project_out(n):
            pe.wait_ge(attn_lo, n + 1)
            for c in range(KC):
                for t, (a, b) in enumerate(PASSES):
                    mm = nc.tensor.matmul(attn_ps[:, 0:D], attn_r[:, a, c * P:(c + 1) * P], attn_w[:, b, 3, c, :],
                                          start=(c == 0 and t == 0), stop=(c == KC - 1 and t == 2))
            mm.then_inc(out_done, 1)

        def qk_read(pair):
            pe.wait_ge(q_hi, pair + 1)
            pe.wait_ge(q_lo, pair + 1)
            pe.wait_ge(k_hi, pair + 1)
            pe.wait_ge(k_lo, pair + 1)

        pe.wait_ge(const_in, 64)
        pe.wait_ge(zeros_set, 5)
        turn_a(0)
        pe.wait_ge(b_scaled, 2)
        lora(0)
        turn_x(0)
        pe.wait_ge(a_out, 1)
        turn_a(1)
        pe.wait_ge(w_hi, 1)
        pe.wait_ge(w_lo, 1)
        project_k(0)
        project_q(0)
        pe.wait_ge(embedded, 2)
        lora(1)
        project_v(0)
        qk_read(0)
        scores(0, 0, 0)
        scores(0, 0, 1)

        def body(i, first=False, following=True, after=True):
            a, b, before = 2 * i, 2 * i + 1, 2 * i - 1
            need(pe, turn_even_out, 4 * i)
            turn_probs(a, 0)
            if following:
                pe.wait_ge(embedded, 2 * i + 4)
            else:
                pe.wait_ge(turn_odd_out, 4 * i)
            turn_probs(a, 1)
            scores(b, 1, 0)
            if following:
                turn_x(i + 1)
            if not first:
                project_out(before)
            pe.wait_ge(turn_even_out, 2 * a + 1)
            turn_probs(a, 2)
            if following:
                project_k(i + 1)
            pe.wait_ge(turn_odd_out, 2 * a + 1)
            turn_probs(a, 3)
            if first:
                pe.wait_ge(a_out, 2)
            turn_recip(a)
            scores(b, 1, 1)
            if following:
                project_q(i + 1)
            attend(a, 0)

            if following:
                pe.wait_ge(q_hi, i + 2)
                pe.wait_ge(q_lo, i + 2)
            else:
                pe.wait_ge(turn_even_out, 2 * a + 2)
            turn_probs(b, 0)
            pe.wait_ge(turn_odd_out, 2 * a + 2)
            turn_probs(b, 1)
            if following:
                qk_read(i + 1)
                scores(b + 1, 0, 0)
            if after:
                pe.wait_ge(attn_normed, a + 1)
                turn_a(i + 2)
            project_out(a)
            if following:
                project_v(i + 1)
            pe.wait_ge(turn_even_out, 2 * b + 1)
            turn_probs(b, 2)
            pe.wait_ge(turn_odd_out, 2 * b + 1)
            turn_probs(b, 3)
            if after:
                pe.wait_ge(a_out, i + 3)
            turn_recip(b)
            if following:
                scores(b + 1, 0, 1)
            if after:
                lora(i + 2)
            attend(b, 1)

        body(0, first=True)
        with pe.Fori(1, PAIRS - 2) as i:
            body(i)
        body(PAIRS - 2, after=False)
        body(PAIRS - 1, following=False, after=False)
        project_out(SEQS - 1)

    @block.vector
    def _(dve):
        def mask_scores(n, *groups):
            for g in groups:
                need_before(dve, w_lo, 1, (scores_done, 4 * n + g + 1), (turned, 4 * n - 3 + g))
                for j in range(4):
                    last = nc.vector.tensor_tensor_reduce(
                        probs[:, 4 * g + j, :], scores_ps[g][:, j * P:(j + 1) * P], mask[:], 1.0, NEVER,
                        ALU.add, ALU.min, neg_max[:, 4 * g + j:4 * g + j + 1])
                last.then_inc(masked, 1)

        def invert_sums(n):
            dve.wait_ge(exps, 4 * n + 4)
            need(dve, recip_turned, n)
            nc.vector.reciprocal(recip[:, 0:HEADS], sums[:]).then_inc(recip_done, 1)

        def turn_recip(n):
            dve.wait_ge(recip_turned, n + 1)
            need(dve, attn_done, n)
            nc.vector.tensor_copy(recip_T[:], attn_ps[0:HEADS, D:D + P]).then_inc(recip_T_out, 1)

        def norm_attention(n):
            dve.wait_ge(attn_done, n + 1)
            nc.vector.tensor_copy(recip_rows[:], attn_ps[:, D:2 * D]).then_inc(recip_rows_out, 1)
            dve.wait_ge(recip_rows_out, n + 1)
            nc.vector.tensor_tensor(attn[:], attn_ps[:, 0:D], recip_rows[:], ALU.mult).then_inc(attn_normed, 1)

        def split_attention(n):
            dve.wait_ge(attn_normed, n + 1)
            need(dve, out_done, n)
            nc.vector.tensor_copy(attn_r[:, 0, :], attn[:]).then_inc(attn_hi, 1)
            dve.wait_ge(attn_hi, n + 1)
            nc.vector.tensor_tensor(attn_r[:, 1, :], attn[:], attn_r[:, 0, :].bitcast(F32),
                                    ALU.subtract).then_inc(attn_lo, 1)

        def low_a(pair):
            dve.wait_ge(a_hi, pair + 1)
            need(dve, lora_done, pair)
            nc.vector.tensor_tensor(a_T[:, 1], attn_ps[:, D:D + 2 * P], a_T[:, 0].bitcast(F32),
                                    ALU.subtract).then_inc(a_out, 1)

        def embed(pair):
            dve.wait_ge(lora_done, pair + 1)
            dve.wait_ge(rows_in, 64 * (pair + 1))
            for s in range(2):
                n = 2 * pair + s
                nc.vector.tensor_tensor(h[:, n, :], turn_ps[1][:, s * D:(s + 1) * D], emb_rows[:, s, :],
                                        ALU.add).then_inc(embedded, 1)
            for s in range(2):
                n = 2 * pair + s
                need_before(dve, w_lo, 1, (embedded, n + 1))
                nc.vector.bn_stats(stats[:, s, :], h[:, n, :]).then_inc(stats_done, 1)

        def average(pair):
            for s in range(2):
                n = 2 * pair + s
                need_before(dve, w_lo, 1, (stats_done, n + 1))
                nc.vector.bn_aggr(mean_var[:, s, :], stats[:, s, :]).then_inc(mv_done, 1)
            dve.wait_ge(mv_done, 2 * pair + 2)
            need(dve, rstd_ready, pair)
            nc.vector.tensor_scalar(var_eps[:], mean_var[:, :, 1], EPS, None, ALU.add).then_inc(eps_added, 1)

        def norm(pair):
            dve.wait_ge(rstd_ready, pair + 1)
            need(dve, x_turned, pair)
            for s in range(2):
                n = 2 * pair + s
                nc.vector.tensor_scalar(xn[:, s, :], h[:, n, :], mean_var[:, s, 0:1], rstd[:, s:s + 1],
                                        ALU.subtract, ALU.mult).then_inc(normed, 1)

        def add_attention(n):
            dve.wait_ge(out_done, n + 1)
            nc.vector.tensor_tensor(h[:, n, :], attn_ps[:, 0:D], h[:, n, :], ALU.add).then_inc(added, 1)

        def copy_turned(n, g):
            dve.wait_ge(turned, 4 * n + g + 1)
            need(dve, attn_done, n)
            nc.vector.tensor_copy(probs_T[:, 4 * g:4 * g + 4, :],
                                  turn_ps[1][:].rearrange("p (j q) -> p j q", j=4)).then_inc(turn_odd_out, 1)

        def low_x(pair):
            dve.wait_ge(x_turned, pair + 1)
            dve.wait_ge(x_hi, pair + 1)
            need(dve, v_done, pair)
            nc.vector.tensor_tensor(xT[:, 1].rearrange("p k n -> p (k n)"), misc_ps[:],
                                    xT[:, 0].rearrange("p k n -> p (k n)").bitcast(F32),
                                    ALU.subtract).then_inc(x_lo, 1)

        def low_q(pair):
            need(dve, scores_done, 8 * pair)
            dve.wait_ge(q_hi, pair + 1)
            nc.vector.scalar_tensor_tensor(out=qT[:, 1], in0=turn_ps[0][:].rearrange("p (c n) -> p c n", c=KC),
                                           scalar=-DK ** -0.5, in1=qT[:, 0].bitcast(F32), op0=ALU.mult,
                                           op1=ALU.subtract).then_inc(q_lo, 1)

        def low_k(pair):
            need(dve, scores_done, 8 * pair)
            dve.wait_ge(k_hi, pair + 1)
            for e in range(2):
                last = nc.vector.scalar_tensor_tensor(
                    out=kT[:, 1, :, e, :], in0=misc_ps[:].rearrange("p (c n) -> p c n", c=KC),
                    scalar=parity[:, e:e + 1], in1=kT[:, 0, :, e, :].bitcast(F32), op0=ALU.mult, op1=ALU.subtract)
            last.then_inc(k_lo, 1)

        dve.wait_ge(b_in, 16)
        dve.wait_ge(zeros_set, 1)
        nc.vector.tensor_scalar(lora_b[:, 0], xn[:, 0, :], LORA_SCALE, None, ALU.mult).then_inc(b_scaled, 1)
        dve.wait_ge(b_scaled, 1)
        nc.vector.scalar_tensor_tensor(out=lora_b[:, 1], in0=xn[:, 0, :], scalar=LORA_SCALE,
                                       in1=lora_b[:, 0].bitcast(F32), op0=ALU.mult,
                                       op1=ALU.subtract).then_inc(b_scaled, 1)
        dve.wait_ge(w_hi, 1)
        nc.vector.tensor_tensor(attn_w[:, 1].rearrange("p w k n -> p (w k n)"), probs[:].rearrange("p a b -> p (a b)"),
                                attn_w[:, 0].rearrange("p w k n -> p (w k n)").bitcast(F32),
                                ALU.subtract).then_inc(w_lo, 1)
        dve.wait_ge(const_in, 64)
        dve.wait_ge(zeros_set, 5)
        dve.wait_ge(w_lo, 1)
        low_a(0)
        embed(0)
        average(0)
        norm(0)
        low_x(0)
        low_a(1)
        low_k(0)
        low_q(0)
        embed(1)
        average(1)
        norm(1)
        mask_scores(0, 0, 1, 2, 3)

        def body(i, first=False, following=True, after=True):
            a, b, before = 2 * i, 2 * i + 1, 2 * i - 1
            if following:
                low_x(i + 1)
            copy_turned(a, 1)
            mask_scores(b, 0)
            if not first:
                add_attention(before)
            invert_sums(a)
            mask_scores(b, 1)
            copy_turned(a, 3)
            turn_recip(a)
            mask_scores(b, 2, 3)
            if following:
                low_q(i + 1)
                low_k(i + 1)

            norm_attention(a)
            split_attention(a)
            copy_turned(b, 1)
            if following:
                mask_scores(b + 1, 0, 1)
            if after:
                low_a(i + 2)
            add_attention(a)
            invert_sums(b)
            copy_turned(b, 3)
            turn_recip(b)
            if following:
                mask_scores(b + 1, 2)
            if after:
                embed(i + 2)
                average(i + 2)
            norm_attention(b)
            if after:
                norm(i + 2)
            split_attention(b)
            if following:
                mask_scores(b + 1, 3)

        body(0, first=True)
        with dve.Fori(1, PAIRS - 2) as i:
            body(i)
        body(PAIRS - 2, after=False)
        body(PAIRS - 1, following=False, after=False)
        add_attention(SEQS - 1)

    @block.scalar
    def _(act):
        def exponents(n, g):
            act.wait_ge(masked, 4 * n + g + 1)
            if g == 0:
                need(act, recip_done, n)
            for j in range(4 * g, 4 * g + 4):
                last = nc.scalar.activation(probs[:, j, :], probs[:, j, :], ACT.Exp, bias=neg_max[:, j:j + 1],
                                            scale=-1.0, accum_out=sums[:, j:j + 1])
            last.then_inc(exps, 1)

        def copy_turned(n, g):
            act.wait_ge(turned, 4 * n + g + 1)
            need(act, attn_done, n)
            nc.scalar.activation(probs_T[:, 4 * g:4 * g + 4, :], turn_ps[0][:].rearrange("p (j q) -> p j q", j=4),
                                 ACT.Copy).then_inc(turn_even_out, 1)

        def widen_v(pair, s):
            act.wait_ge(v_done, pair + 1)
            need(act, attn_done, 2 * pair - 1 + s)
            for e in range(2):
                last = nc.scalar.activation(
                    v_wide[:, s].rearrange("p (j e) w -> p j e w", e=2)[:, :, e, e * DK:(e + 1) * DK],
                    misc_ps[:, s * D:(s + 1) * D].rearrange("p (x e w) -> p x e w", e=2, w=DK)[:, :, e, :], ACT.Copy)
            if s == 1:
                last.then_inc(v_out, 1)

        def high_a(pair, out_before):
            act.wait_ge(a_turned, pair + 1)
            need(act, out_done, out_before)
            need(act, lora_done, pair)
            nc.scalar.activation(a_T[:, 0], attn_ps[:, D:D + 2 * P], ACT.Copy).then_inc(a_hi, 1)

        def high_x(pair):
            act.wait_ge(x_turned, pair + 1)
            need(act, v_done, pair)
            nc.scalar.activation(xT[:, 0].rearrange("p k n -> p (k n)"), misc_ps[:], ACT.Copy).then_inc(x_hi, 1)

        def high_q(pair):
            act.wait_ge(q_done, pair + 1)
            need(act, scores_done, 8 * pair)
            nc.scalar.activation(qT[:, 0], turn_ps[0][:].rearrange("p (c n) -> p c n", c=KC), ACT.Copy,
                                 scale=-DK ** -0.5).then_inc(q_hi, 1)

        def high_k(pair):
            act.wait_ge(k_done, pair + 1)
            need(act, scores_done, 8 * pair)
            for e in range(2):
                last = nc.scalar.activation(kT[:, 0, :, e, :], misc_ps[:].rearrange("p (c n) -> p c n", c=KC),
                                            ACT.Copy, scale=parity[:, e:e + 1])
            last.then_inc(k_hi, 1)

        high_a(0, 0)
        act.wait_ge(w_in, 16)
        nc.scalar.activation(attn_w[:, 0].rearrange("p w k n -> p (w k n)"), probs[:].rearrange("p a b -> p (a b)"),
                             ACT.Copy).then_inc(w_hi, 1)
        act.wait_ge(const_in, 64)
        act.wait_ge(zeros_set, 5)
        high_x(0)
        high_a(1, 0)
        high_k(0)
        high_q(0)
        widen_v(0, 0)
        widen_v(0, 1)
        exponents(0, 0)
        exponents(0, 1)

        def body(i, following=True, after=True):
            a, b = 2 * i, 2 * i + 1
            copy_turned(a, 0)
            exponents(a, 2)
            if following:
                high_x(i + 1)
            exponents(a, 3)
            copy_turned(a, 2)
            exponents(b, 0)
            if following:
                high_k(i + 1)
                high_q(i + 1)
            exponents(b, 1)

            copy_turned(b, 0)
            exponents(b, 2)
            exponents(b, 3)
            if after:
                high_a(i + 2, a + 1)
            copy_turned(b, 2)
            if following:
                exponents(b + 1, 0)
                widen_v(i + 1, 0)
                exponents(b + 1, 1)
                widen_v(i + 1, 1)

        body(0)
        with act.Fori(1, PAIRS - 2) as i:
            body(i)
        body(PAIRS - 2, after=False)
        body(PAIRS - 1, following=False, after=False)


def expert_block(nc, ctx, h, ffn_hi, ffn_lo, ident, router_d, bias_d, sel_d, out_d):
    def sb(name, shape, dt=F32):
        return ctx.enter_context(nc.sbuf_tensor(name, shape, dt))

    def bank(name):
        return ctx.enter_context(nc.psum_tensor(name, [P, 512], F32))

    def sem(name):
        return ctx.enter_context(nc.semaphore(name))

    parts = [w[:].rearrange("p (t n) -> p t n", t=3) for w in (ffn_hi, ffn_lo)]
    gate_w = [w[:, 0, :].rearrange("p (k n) -> p k n", k=KC) for w in parts]
    up_w = [w[:, 1, :].rearrange("p (k n) -> p k n", k=KC) for w in parts]
    down_w = [w[:, 2, :].rearrange("p (c n) -> p c n", c=CH) for w in parts]

    router_raw = sb("router_raw", [P, KC, P])
    router_w = sb("router_w", [P, 2, KC, P], F32R)
    expert_sel_raw = sb("expert_sel_raw", [2 * E, CH_ROUTED, P])
    expert_sel = sb("expert_sel", [2 * E, CH_ROUTED, P], F32R)
    bias = sb("bias", [P, E])
    earlier = sb("earlier", [P, E, E])
    minus_half = sb("minus_half2", [P, GT])
    stats = sb("stats2", [P, GT, 6])
    mean_var = sb("mean_var2", [P, GT, 2])
    var_eps = sb("var_eps2", [P, GT])
    rstd = sb("rstd2", [P, GT])
    xn = sb("xn2", [P, GT, D])
    xT = sb("xT2", [P, 2, 2, KC, TOK], F32R)
    score_T = sb("score_T", [E, TOK])
    score = sb("score", [P, GT, E])
    biased = sb("biased", [P, GT, E])
    pair_sums = sb("pair_sums", [P, GT, EG, 6])
    group_score = sb("group_score", [P, GT, EG])
    beats = sb("beats", [P, E, E])
    ties = sb("ties", [P, E, E])
    group_rank = sb("group_rank", [P, GT, EG])
    group_on = sb("group_on", [P, GT, EG])
    group_off = sb("group_off", [P, GT, EG])
    candidates = sb("candidates", [P, GT, E])
    rank = sb("rank", [P, GT, E])
    weight = sb("weight", [P, GT, E])
    total = sb("total", [P, GT])
    total_inv = sb("total_inv", [P, GT])
    combine = sb("combine", [P, GT, E])
    combine_hi = sb("combine_hi", [P, GT, E], F32R)
    combine_r = sb("combine_r", [P, GT, P])
    combine_T = sb("combine_T", [2 * E, TOK], F32R)
    silu = sb("silu", [P, 2, TOK])
    scaled = sb("scaled", [P, 2, TOK])
    hid = sb("hid", [P, 2, TOK])
    hid_hi = sb("hid_hi", [P, 2, TOK], F32R)
    hid_lo = sb("hid_lo", [P, 2, TOK], F32R)

    gate_ps = [bank(f"gate_ps{k}") for k in range(2)]
    up_ps = [bank(f"up_ps{k}") for k in range(2)]
    combine_ps = bank("combine_ps")
    out_ps = [bank(f"out_ps{k}") for k in range(2)]
    misc_ps = bank("misc_ps2")

    const_in, stored = sem("const2_in"), sem("stored")
    zeros_set, rstd_ready = sem("zeros2_set"), sem("rstd2_ready")
    x_turned, logits_done, score_turned, combine_turned = (sem("x2_turned"), sem("logits_done"), sem("score_turned"),
                                                           sem("combine_turned"))
    gate_done, up_done, spread_done, down_done = sem("gate_done"), sem("up_done"), sem("spread_done"), sem("down_done")
    router_lo, eps_added, normed, x_lo = sem("router_lo"), sem("eps2_added"), sem("normed2"), sem("x2_lo")
    combine_hi_done = sem("combine_hi_done")
    step, score_out, combined, scaled_done = sem("step"), sem("score_out"), sem("combined"), sem("scaled_done")
    hid_done, hid_lo_done, y_done = sem("hid_done"), sem("hid_lo_done"), sem("y_done")
    consts_cast, x_hi, scored, combine_T_out = sem("consts_cast"), sem("x2_hi"), sem("scored"), sem("combine_T_out")
    silu_done, hid_hi_done = sem("silu_done"), sem("hid_hi_done")

    block = ctx.enter_context(nc.Block())
    out_rows = out_d.rearrange("(t p) d -> p t d", p=P)


    @block.sync
    def _(sp):
        sp.dma_start(router_raw[:], router_d).then_inc(const_in, 16)
        sp.dma_start(expert_sel_raw[:], sel_d).then_inc(const_in, 16)
        sp.dma_start(bias[:], bias_d).then_inc(const_in, 16)

        with sp.Fori(0, GROUPS) as g:
            sp.wait_ge(y_done, 2 * g + 2)
            sp.dma_start(out_rows[:, bass.ds(GT * g, GT), :], h[:, bass.ds(GT * g, GT), :]).then_inc(stored, 16)
        sp.wait_ge(stored, 16 * GROUPS)

    @block.gpsimd
    def _(pool):
        nc.gpsimd.memset(combine_r[:], 0.0).then_inc(zeros_set, 1)
        nc.gpsimd.memset(minus_half[:], -0.5).then_inc(zeros_set, 1)
        nc.gpsimd.memset(earlier[:], 1.0).then_inc(zeros_set, 1)
        pool.wait_ge(zeros_set, 3)
        nc.gpsimd.affine_select(out=earlier[:], in_=earlier[:], compare_op=ALU.is_gt, fill=0.0, base=0,
                                pattern=[[1, E], [-1, E]], channel_multiplier=0).then_inc(zeros_set, 1)

        def root(g):
            pool.wait_ge(eps_added, g + 1)
            nc.gpsimd.tensor_tensor(rstd[:], var_eps[:], minus_half[:], ALU.pow).then_inc(rstd_ready, 1)

        with pool.Fori(0, GROUPS) as g:
            root(g)

    @block.tensor
    def _(pe):
        def turn_x(g, k):
            pe.wait_ge(normed, g + 1)
            if k == 0:
                need(pe, combine_T_out, g)
            else:
                pe.wait_ge(x_hi, 2 * g + 1)
                pe.wait_ge(x_lo, 2 * g + 1)
            for t in range(GT):
                mm = nc.tensor.transpose(misc_ps[:, t * P:(t + 1) * P], xn[:, t, k * P:(k + 1) * P], ident[:])
            mm.then_inc(x_turned, 1)

        def logits(g, parity):
            pe.wait_ge(x_hi, 2 * g + 2)
            pe.wait_ge(x_lo, 2 * g + 2)
            for k in range(KC):
                for n, (a, b) in enumerate(PASSES):
                    mm = nc.tensor.matmul(misc_ps[:], router_w[:, a, k, :], xT[:, parity, b, k, :],
                                          start=(k == 0 and n == 0), stop=(k == KC - 1 and n == 2))
            mm.then_inc(logits_done, 1)

        def turn_scores(g):
            need_before(pe, zeros_set, 4, (scored, g + 1))
            for t in range(GT):
                mm = nc.tensor.transpose(misc_ps[:, t * E:(t + 1) * E], score_T[:, t * P:(t + 1) * P],
                                         ident[0:E, 0:E])
            mm.then_inc(score_turned, 1)

        def turn_combine(g):
            pe.wait_ge(combined, g + 1)
            pe.wait_ge(score_out, g + 1)
            for t in range(GT):
                mm = nc.tensor.transpose(misc_ps[:, t * P:(t + 1) * P], combine_r[:, t, :], ident[:])
            mm.then_inc(combine_turned, 1)

        def spread(g, c):
            if c == 0:
                pe.wait_ge(combine_T_out, g + 1)
            need(pe, scaled_done, CH_ROUTED * g + c)
            nc.tensor.matmul(combine_ps[:], expert_sel[:, c, :], combine_T[:], start=True,
                             stop=True).then_inc(spread_done, 1)

        def up_or_gate(g, parity, c, w, ps):
            for k in range(KC):
                for n, (a, b) in enumerate(PASSES):
                    mm = nc.tensor.matmul(ps[:], w[a][:, k, c * P:(c + 1) * P], xT[:, parity, b, k, :],
                                          start=(k == 0 and n == 0), stop=(k == KC - 1 and n == 2))
            return mm

        def down(g, p):
            pe.wait_ge(hid_hi_done, CH * g + p + 1)
            pe.wait_ge(hid_lo_done, CH * g + p + 1)
            hid_r = (hid_hi, hid_lo)
            for t in range(GT):
                if p == 0 and t % 2 == 0:
                    need(pe, y_done, 2 * g - 1 + t // 2)
                for n, (a, b) in enumerate(PASSES):
                    mm = nc.tensor.matmul(out_ps[t // 2][:, (t % 2) * D:(t % 2 + 1) * D],
                                          hid_r[a][:, p % 2, t * P:(t + 1) * P], down_w[b][:, CHUNKS[p], :],
                                          start=(p == 0 and n == 0 and t % 2 == 0),
                                          stop=(p == CH - 1 and n == 2), skip_group_check=True)
            mm.then_inc(down_done, 1)

        def experts(g, parity, first=False, routes=True):
            at = START if first else STEADY
            for p, c in enumerate(CHUNKS):
                need(pe, silu_done, CH * g + p - 1)
                up_or_gate(g, parity, c, gate_w, gate_ps[p % 2]).then_inc(gate_done, 1)
                if p == SHARED and first:
                    turn_combine(g)
                elif c < CH_ROUTED:
                    spread(g, c)
                need(pe, hid_done, CH * g + p - 1)
                up_or_gate(g, parity, c, up_w, up_ps[p % 2]).then_inc(up_done, 1)
                if p == 0 and not first:
                    turn_combine(g)
                if p == SHARED and first:
                    spread(g, c)
                if routes and p in at["turned"]:
                    turn_x(g + 1, at["turned"].index(p))
                if routes and p == at["logits"]:
                    logits(g + 1, 1 - parity)
                if routes and p == at["scores"]:
                    turn_scores(g + 1)
                if p > 0:
                    down(g, p - 1)
                elif not first:
                    down(g - 1, CH - 1)

        pe.wait_ge(zeros_set, 4)
        turn_x(0, 0)
        turn_x(0, 1)
        pe.wait_ge(consts_cast, 2)
        pe.wait_ge(router_lo, 1)
        logits(0, 0)
        turn_scores(0)
        experts(0, 0, first=True)
        with pe.Fori(0, GROUPS // 2 - 1) as j:
            experts(2 * j + 1, 1)
            experts(2 * j + 2, 0)
        experts(GROUPS - 1, 1, routes=False)
        down(GROUPS - 1, CH - 1)

    @block.vector
    def _(dve):
        STEPS = 18 + 4 * GT


        def measure_rows(g):
            for t in range(GT):
                last = nc.vector.bn_stats(stats[:, t, :], h[:, GT * g + t, :])
            last.then_inc(step, 1)

        def average_rows(g):
            need_before(dve, zeros_set, 4, (step, STEPS * g + 1))
            for t in range(GT):
                last = nc.vector.bn_aggr(mean_var[:, t, :], stats[:, t, :])
            last.then_inc(step, 1)
            dve.wait_ge(step, STEPS * g + 2)
            nc.vector.tensor_scalar(var_eps[:], mean_var[:, :, 1], EPS, None, ALU.add).then_inc(eps_added, 1)

        def norm_rows(g):
            dve.wait_ge(rstd_ready, g + 1)
            need(dve, x_turned, 2 * g)
            for t in range(GT):
                last = nc.vector.tensor_scalar(xn[:, t, :], h[:, GT * g + t, :], mean_var[:, t, 0:1],
                                               rstd[:, t:t + 1], ALU.subtract, ALU.mult)
            last.then_inc(normed, 1)

        def low_x(g, parity, k):
            dve.wait_ge(x_turned, 2 * g + k + 1)
            dve.wait_ge(x_hi, 2 * g + k + 1)
            nc.vector.tensor_tensor(xT[:, parity, 1, k, :], misc_ps[:], xT[:, parity, 0, k, :].bitcast(F32),
                                    ALU.subtract).then_inc(x_lo, 1)


        def steps_from(g, first):
            done = [first]

            def then(last):
                done[0] += 1
                last.then_inc(step, 1)
                dve.wait_ge(step, STEPS * g + done[0])
            return then

        def score_groups(g):
            tt = nc.vector.tensor_tensor
            dve.wait_ge(score_turned, g + 1)
            nc.vector.tensor_copy(score[:], misc_ps[:, 0:GT * E].rearrange("p (t e) -> p t e", t=GT)
                                  ).then_inc(score_out, 1)
            dve.wait_ge(score_out, g + 1)
            then = steps_from(g, 2)
            then(tt(biased[:], score[:], bias[:].unsqueeze(1).to_broadcast([P, GT, E]), ALU.add))
            b4 = biased[:].rearrange("p t (g i) -> p t g i", g=EG)
            at = 0
            for d in (1, 2, 3):
                last = tt(pair_sums[:, :, :, at:at + 4 - d], b4[:, :, :, 0:4 - d], b4[:, :, :, d:4], ALU.add)
                at += 4 - d
            then(last)
            then(nc.vector.tensor_reduce(group_score[:], pair_sums[:], AX_X, ALU.max))

        def rank_groups(g):
            tt = nc.vector.tensor_tensor
            then = steps_from(g, 5)
            gs = group_score[:]
            gi = gs.unsqueeze(3).to_broadcast([P, GT, EG, EG])
            gj = gs.unsqueeze(2).to_broadcast([P, GT, EG, EG])
            more = beats[:].rearrange("p (t i) (j) -> p t i j", t=GT)[:, :, :, 0:EG]
            same = ties[:].rearrange("p (t i) (j) -> p t i j", t=GT)[:, :, :, 0:EG]
            early = earlier[:, 0:EG, 0:EG].unsqueeze(1).to_broadcast([P, GT, EG, EG])
            tt(more, gj, gi, ALU.is_gt)
            then(tt(same, gj, gi, ALU.is_equal))
            then(tt(same, same, early, ALU.mult))
            then(tt(more, more, same, ALU.add))
            then(nc.vector.tensor_reduce(group_rank[:], more, AX_X, ALU.add))

        def mark_candidates(g):
            tt = nc.vector.tensor_tensor
            then = steps_from(g, 9)
            nc.vector.tensor_scalar(group_on[:], group_rank[:], 1.5, None, ALU.is_lt)
            then(nc.vector.tensor_scalar(group_off[:], group_rank[:], 1.5, -NEVER, ALU.is_gt, ALU.mult))
            b4 = biased[:].rearrange("p t (g i) -> p t g i", g=EG)
            c4 = candidates[:].rearrange("p t (g i) -> p t g i", g=EG)
            then(tt(c4, b4, group_on[:].unsqueeze(3).to_broadcast([P, GT, EG, 4]), ALU.mult))
            then(tt(c4, c4, group_off[:].unsqueeze(3).to_broadcast([P, GT, EG, 4]), ALU.add))

        def compare_experts(g, t):
            tt = nc.vector.tensor_tensor
            then = steps_from(g, 12 + 4 * t)
            ci = candidates[:, t, :].unsqueeze(2).to_broadcast([P, E, E])
            cj = candidates[:, t, :].unsqueeze(1).to_broadcast([P, E, E])
            tt(beats[:], cj, ci, ALU.is_gt)
            then(tt(ties[:], cj, ci, ALU.is_equal))

        def rank_experts(g, t):
            tt = nc.vector.tensor_tensor
            then = steps_from(g, 13 + 4 * t)
            then(tt(ties[:], ties[:], earlier[:], ALU.mult))
            then(tt(beats[:], beats[:], ties[:], ALU.add))
            then(nc.vector.tensor_reduce(rank[:, t, :], beats[:], AX_X, ALU.add))

        def weigh(g):
            then = steps_from(g, 12 + 4 * GT)
            then(nc.vector.tensor_scalar(rank[:], rank[:], 3.5, None, ALU.is_lt))
            then(nc.vector.tensor_tensor(weight[:], score[:], rank[:], ALU.mult))
            then(nc.vector.tensor_reduce(total[:], weight[:], AX_X, ALU.add))
            then(nc.vector.tensor_scalar(total[:], total[:], 1e-20, None, ALU.add))
            then(nc.vector.reciprocal(total_inv[:], total[:]))

        def split_weights(g):
            then = steps_from(g, 17 + 4 * GT)
            need(dve, combine_turned, g)
            then(nc.vector.tensor_tensor(combine[:], weight[:], total_inv[:].unsqueeze(2).to_broadcast([P, GT, E]),
                                         ALU.mult))
            nc.vector.tensor_copy(combine_hi[:], combine[:]).then_inc(combine_hi_done, 1)
            dve.wait_ge(combine_hi_done, g + 1)
            nc.vector.tensor_copy(combine_r[:, :, 0:E], combine_hi[:].bitcast(F32))
            nc.vector.tensor_tensor(combine_r[:, :, E:2 * E], combine[:], combine_hi[:].bitcast(F32),
                                    ALU.subtract).then_inc(combined, 1)

        def hidden(g, p):
            n = CH * g + p
            dve.wait_ge(silu_done, n + 1)
            if p >= SHARED:
                c = CHUNKS[p]
                dve.wait_ge(spread_done, CH_ROUTED * g + c + 1)
                nc.vector.tensor_tensor(scaled[:, p % 2, :], combine_ps[:], silu[:, p % 2, :],
                                        ALU.mult).then_inc(scaled_done, 1)
                dve.wait_ge(scaled_done, CH_ROUTED * g + c + 1)
                left = scaled
            else:
                left = silu
            dve.wait_ge(up_done, n + 1)
            need(dve, hid_hi_done, n - 1)
            nc.vector.tensor_tensor(hid[:, p % 2, :], up_ps[p % 2][:], left[:, p % 2, :], ALU.mult
                                    ).then_inc(hid_done, 1)

        def low_hidden(g, p):
            n = CH * g + p
            dve.wait_ge(hid_done, n + 1)
            dve.wait_ge(hid_hi_done, n + 1)
            nc.vector.tensor_tensor(hid_lo[:, p % 2, :], hid[:, p % 2, :], hid_hi[:, p % 2, :].bitcast(F32),
                                    ALU.subtract).then_inc(hid_lo_done, 1)

        def finish(g):
            dve.wait_ge(down_done, CH * g + CH)
            for k in range(2):
                rows = h[:, bass.ds(GT * g + 2 * k, 2), :]
                nc.vector.tensor_tensor(rows, out_ps[k][:].rearrange("p (t d) -> p t d", t=2), rows,
                                        ALU.add).then_inc(y_done, 1)

        def experts(g, parity, first=False, routes=True):
            at = START if first else STEADY
            for p in range(CH):
                hidden(g, p)
                if routes:
                    if p == at["normed"] - 1 and not first:
                        measure_rows(g + 1)
                    if p == at["normed"]:
                        if first:
                            measure_rows(g + 1)
                        average_rows(g + 1)
                    if p == at["scores"]:
                        score_groups(g + 1)
                    if p == at["candidates"]:
                        mark_candidates(g + 1)
                    if p in at["ranked"]:
                        compare_experts(g + 1, at["ranked"].index(p))
                    if p == at["weighed"] and not first:
                        weigh(g + 1)
                low_hidden(g, p)
                if first and p + 1 < GT:
                    compare_experts(0, p + 1)
                    rank_experts(0, p + 1)
                if first and p == OWN_WEIGHED:
                    weigh(0)
                    split_weights(0)
                if p == 0 and not first:
                    finish(g - 1)
                if routes:
                    if p == at["normed"]:
                        norm_rows(g + 1)
                    if p in at["turned"]:
                        low_x(g + 1, 1 - parity, at["turned"].index(p))
                    if p == at["scores"]:
                        rank_groups(g + 1)
                    if p in at["ranked"]:
                        rank_experts(g + 1, at["ranked"].index(p))
                    if p == at["weighed"]:
                        if first:
                            weigh(g + 1)
                        split_weights(g + 1)

        dve.wait_ge(zeros_set, 4)
        measure_rows(0)
        average_rows(0)
        norm_rows(0)
        dve.wait_ge(const_in, 48)
        dve.wait_ge(consts_cast, 2)
        nc.vector.tensor_tensor(router_w[:, 1], router_raw[:], router_w[:, 0].bitcast(F32),
                                ALU.subtract).then_inc(router_lo, 1)
        low_x(0, 0, 0)
        low_x(0, 0, 1)
        score_groups(0)
        rank_groups(0)
        mark_candidates(0)
        compare_experts(0, 0)
        rank_experts(0, 0)
        experts(0, 0, first=True)
        with dve.Fori(0, GROUPS // 2 - 1) as j:
            experts(2 * j + 1, 1)
            experts(2 * j + 2, 0)
        experts(GROUPS - 1, 1, routes=False)
        finish(GROUPS - 1)

    @block.scalar
    def _(act):
        def high_x(g, parity, k):
            act.wait_ge(x_turned, 2 * g + k + 1)
            need(act, up_done, CH * (g - 1))
            nc.scalar.activation(xT[:, parity, 0, k, :], misc_ps[:], ACT.Copy).then_inc(x_hi, 1)

        def score_rows(g):
            act.wait_ge(logits_done, g + 1)
            nc.scalar.activation(score_T[:], misc_ps[0:E, :], ACT.Sigmoid).then_inc(scored, 1)

        def copy_combine(g):
            act.wait_ge(combine_turned, g + 1)
            need(act, spread_done, CH_ROUTED * g)
            nc.scalar.activation(combine_T[:], misc_ps[0:2 * E, :], ACT.Copy).then_inc(combine_T_out, 1)

        def gated(g, p):
            act.wait_ge(gate_done, CH * g + p + 1)
            need(act, hid_done, CH * g + p - 1)
            nc.scalar.activation(silu[:, p % 2, :], gate_ps[p % 2][:], ACT.Silu).then_inc(silu_done, 1)

        def high_hidden(g, p):
            act.wait_ge(hid_done, CH * g + p + 1)
            need(act, down_done, CH * g + p - 1)
            nc.scalar.activation(hid_hi[:, p % 2, :], hid[:, p % 2, :], ACT.Copy).then_inc(hid_hi_done, 1)

        def experts(g, parity, first=False, routes=True):
            at = START if first else STEADY
            for p in range(CH):
                gated(g, p)
                if p == (SHARED if first else 0):
                    copy_combine(g)
                high_hidden(g, p)
                if routes and p in at["turned"]:
                    high_x(g + 1, 1 - parity, at["turned"].index(p))
                if routes and p == at["logits"]:
                    score_rows(g + 1)

        act.wait_ge(const_in, 48)
        nc.scalar.activation(router_w[:, 0], router_raw[:], ACT.Copy).then_inc(consts_cast, 1)
        nc.scalar.activation(expert_sel[:], expert_sel_raw[:], ACT.Copy).then_inc(consts_cast, 1)
        high_x(0, 0, 0)
        high_x(0, 0, 1)
        score_rows(0)
        experts(0, 0, first=True)
        with act.Fori(0, GROUPS // 2 - 1) as j:
            experts(2 * j + 1, 1)
            experts(2 * j + 2, 0)
        experts(GROUPS - 1, 1, routes=False)




def kernel(x, L0_tok_W, L0_tok_A, L0_tok_B, L0_attn_q_heads, L0_attn_k_heads, L0_attn_v_heads, L0_attn_output_proj,
           L0_ffn_router_w, L0_ffn_correction_bias, L0_ffn_gate_w, L0_ffn_up_w, L0_ffn_down_w, L0_ffn_shared_gate_w,
           L0_ffn_shared_up_w, L0_ffn_shared_down_w):
    from concourse import bacc
    from concourse.bass_utils import run_bass_kernel_spmd

    def chunked(w):
        return np.concatenate(np.split(w, w.shape[0] // P), axis=1)

    attn_w = [chunked(np.asarray(w).T) for w in (L0_attn_q_heads, L0_attn_k_heads, L0_attn_v_heads,
                                                 L0_attn_output_proj)]

    def by_channel(w, shared):
        return chunked(np.concatenate([np.asarray(w).transpose(1, 0, 2).reshape(D, -1), np.asarray(shared).T], axis=1))

    down = np.concatenate([np.asarray(L0_ffn_down_w).reshape(-1, D), np.asarray(L0_ffn_shared_down_w).T], axis=0)
    ffn_w = np.concatenate([by_channel(L0_ffn_gate_w, L0_ffn_shared_gate_w),
                            by_channel(L0_ffn_up_w, L0_ffn_shared_up_w), chunked(down)], axis=1)
    router = np.zeros((KC, P, P), np.float32)
    router[:, :, 0:E] = np.asarray(L0_ffn_router_w).T.reshape(KC, P, E)

    const = np.zeros((P, P + 2 + KC * P), np.float32)
    rows, cols = np.indices((P, P))
    const[:, 0:P] = np.where(cols > rows, np.float32(NEVER), np.float32(0))
    odd = np.arange(P) // DK % 2
    const[:, P] = odd == 0
    const[:, P + 1] = odd == 1
    for c in range(KC):
        for r in range(P):
            const[slot(r // 32, c, r // DK % 2), P + 2 + c * P + r] = 1
    sel = np.zeros((2 * E, CH_ROUTED, P), np.float32)
    for c in range(CH_ROUTED):
        for m in range(P):
            sel[2 * c + m // 64, c, m] = 1
            sel[E + 2 * c + m // 64, c, m] = 1

    arrays = {
        "idx": np.ascontiguousarray(np.asarray(x).T),
        "emb": np.ascontiguousarray(L0_tok_W),
        "lora_a": np.ascontiguousarray(L0_tok_A),
        "lora_b": np.ascontiguousarray(L0_tok_B),
        "attn_w": np.ascontiguousarray(np.concatenate(attn_w, axis=1)),
        "ffn_w": np.ascontiguousarray(ffn_w),
        "router": np.ascontiguousarray(router.transpose(1, 0, 2)),
        "bias": np.ascontiguousarray(np.broadcast_to(np.asarray(L0_ffn_correction_bias), (P, E))),
        "ident": np.eye(P, dtype=np.float32),
        "const": const,
        "sel": sel,
    }
    nc = bacc.Bacc("TRN2", target_bir_lowering=False, num_devices=1)
    args = [nc.dram_tensor(f"in_{name}", a.shape, mybir.dt.from_np(a.dtype), kind="ExternalInput").ap()
            for name, a in arrays.items()]
    out = nc.dram_tensor("out", (SEQS * P, D), F32, kind="ExternalOutput").ap()
    build(nc, *args, out)
    r = run_bass_kernel_spmd(nc, [{f"in_{name}": a for name, a in arrays.items()}], core_ids=[0])
    return r.results[0]["out"].reshape(SEQS, P, D)
```
